# Optimizing a Trainium2 kernel written in Bass

```python
import numpy as np
import jax
import jax.numpy as jnp

def _softmax(x, axis=-1):
    return jax.nn.softmax(x, axis=axis)

def _gelu(x):
    return jax.nn.gelu(x, approximate=True)

def _silu(x):
    return jax.nn.silu(x)

def _sigmoid(x):
    return jax.nn.sigmoid(x)

def _layernorm(x, axis=-1, eps=1e-05):
    m = jnp.mean(x, axis=axis, keepdims=True)
    v = jnp.var(x, axis=axis, keepdims=True)
    return (x - m) / jnp.sqrt(v + eps)

def _scatter_add(tgt, idx, src, axis=0):
    return tgt.at[idx].add(src)

def _segment_sum(src, seg, n):
    return jax.ops.segment_sum(src, seg, n)
kernel_name = 'mk_gnn_preln_d2_gnn_r8_deb6c0'

def setup_inputs(seed: int=0):
    np.random.seed(seed)
    _w = jnp.asarray

    def _rec_inputs():
        import jax
        import jax.numpy as jnp
        _gk = jax.random.key(seed)
        x = -0.0006008 + 1.001 * jax.random.normal(jax.random.fold_in(_gk, 1), (6250, 256), jnp.float32)
        src = jax.random.randint(jax.random.fold_in(_gk, 2), (200000,), 0, 6250, jnp.int32)
        dst = jax.random.randint(jax.random.fold_in(_gk, 3), (200000,), 0, 6250, jnp.int32)
        _o = jnp.argsort(dst, stable=True)
        src = src[_o]
        dst = dst[_o]
        edge_weight = jax.random.uniform(jax.random.fold_in(_gk, 12), (200000,), jnp.float32, 0.0, 1)
        return (x, src, dst, edge_weight)
    x, src, dst, edge_weight = _rec_inputs()

    def _L0_gnn_setup():
        import jax, jax.numpy as jnp
        import numpy as np
        N_NODES = 1250
        N_EDGES = 40000
        D = 256
        key = jax.random.key(seed)
        k1, k2, k3, k4, k5 = jax.random.split(key, 5)
        x = jax.random.normal(k1, (N_NODES, D), dtype=jnp.float32)
        src = jax.random.randint(k2, (N_EDGES,), 0, N_NODES, dtype=jnp.int32)
        dst = jax.random.randint(k3, (N_EDGES,), 0, N_NODES, dtype=jnp.int32)
        s = 1.0 / np.sqrt(D)
        theta_w = jax.random.uniform(k4, (D, D), jnp.float32, -s, s)
        theta_b = jnp.zeros((D,), jnp.float32)
        phi_w = jax.random.uniform(k5, (D, D), jnp.float32, -s, s)
        phi_b = jnp.zeros((D,), jnp.float32)
        return {'x': x, 'src': src, 'dst': dst, 'theta_w': theta_w, 'theta_b': theta_b, 'phi_w': phi_w, 'phi_b': phi_b}
    _L0_gnn_all = _L0_gnn_setup()
    _L0_gnn_in = {k: v for k, v in _L0_gnn_all.items() if k in ('theta_w', 'theta_b', 'phi_w', 'phi_b')}
    del _L0_gnn_all

    def _L1_gnn_setup():
        import jax, jax.numpy as jnp
        import numpy as np
        N_NODES = 12500
        N_EDGES = 400000
        DIM_IN = 256
        DIM_OUT = 256
        key = jax.random.key(seed)
        ks = jax.random.split(key, 8)
        feat_in = jax.random.normal(ks[0], (N_NODES, DIM_IN), dtype=jnp.float32)
        edge_row = jax.random.randint(ks[1], (N_EDGES,), 0, N_NODES, dtype=jnp.int32)
        edge_col = jax.random.randint(ks[2], (N_EDGES,), 0, N_NODES, dtype=jnp.int32)
        edge_val = jax.random.uniform(ks[3], (N_EDGES,), dtype=jnp.float32)
        s1 = 1.0 / np.sqrt(DIM_IN)
        s2 = 1.0 / np.sqrt(DIM_OUT)
        W1 = jax.random.normal(ks[4], (DIM_IN, DIM_OUT), dtype=jnp.float32) * s1
        b1 = jnp.zeros((DIM_OUT,), dtype=jnp.float32)
        W2 = jax.random.normal(ks[5], (DIM_OUT, DIM_OUT), dtype=jnp.float32) * s2
        b2 = jnp.zeros((DIM_OUT,), dtype=jnp.float32)
        eps = jnp.zeros((1,), dtype=jnp.float32)
        offset = jnp.zeros((DIM_OUT,), dtype=jnp.float32)
        scale = jnp.ones((DIM_OUT,), dtype=jnp.float32)
        return {'feat_in': feat_in, 'edge_row': edge_row, 'edge_col': edge_col, 'edge_val': edge_val, 'W1': W1, 'b1': b1, 'W2': W2, 'b2': b2, 'eps': eps, 'offset': offset, 'scale': scale}
    _L1_gnn_all = _L1_gnn_setup()
    _L1_gnn_in = {k: v for k, v in _L1_gnn_all.items() if k in ('W1', 'b1', 'W2', 'b2', 'eps', 'offset', 'scale')}
    del _L1_gnn_all
    return {'x': x, 'src': src, 'dst': dst, 'edge_weight': edge_weight, 'L0_gnn_theta_w': _L0_gnn_in['theta_w'], 'L0_gnn_theta_b': _L0_gnn_in['theta_b'], 'L0_gnn_phi_w': _L0_gnn_in['phi_w'], 'L0_gnn_phi_b': _L0_gnn_in['phi_b'], 'L1_gnn_W1': _L1_gnn_in['W1'], 'L1_gnn_b1': _L1_gnn_in['b1'], 'L1_gnn_W2': _L1_gnn_in['W2'], 'L1_gnn_b2': _L1_gnn_in['b2'], 'L1_gnn_eps': _L1_gnn_in['eps'], 'L1_gnn_offset': _L1_gnn_in['offset'], 'L1_gnn_scale': _L1_gnn_in['scale']}

def reference(x, src, dst, edge_weight, L0_gnn_theta_w, L0_gnn_theta_b, L0_gnn_phi_w, L0_gnn_phi_b, L1_gnn_W1, L1_gnn_b1, L1_gnn_W2, L1_gnn_b2, L1_gnn_eps, L1_gnn_offset, L1_gnn_scale):
    import jax
    import jax.numpy as jnp

    def _L0_gnn_ref(x, src, dst, theta_w, theta_b, phi_w, phi_b):
        import jax, jax.numpy as jnp
        import numpy as np
        N_NODES = 1250
        N_EDGES = 40000
        D = 256
        x_src = x[src]
        x_dst = x[dst]
        theta_x = (x_dst - x_src) @ theta_w.T + theta_b
        phi_x = x_src @ phi_w.T + phi_b
        e = jax.nn.relu(theta_x + phi_x)
        out = jax.ops.segment_max(e, dst, num_segments=x.shape[0])
        return jnp.where(jnp.isfinite(out), out, 0.0)

    def _L1_gnn_ref(feat_in, edge_row, edge_col, edge_val, W1, b1, W2, b2, eps, offset, scale):
        import jax, jax.numpy as jnp
        import numpy as np
        N_NODES = 12500
        N_EDGES = 400000
        DIM_IN = 256
        DIM_OUT = 256
        msg = edge_val[:, None] * feat_in[edge_col]
        aggr = jax.ops.segment_sum(msg, edge_row, num_segments=feat_in.shape[0])
        aggr = aggr + (1.0 + eps) * feat_in
        h = jnp.maximum(aggr @ W1 + b1, 0.0) @ W2 + b2
        h = jnp.maximum(h, 0.0)
        mean = jnp.mean(h, axis=1, keepdims=True)
        var = jnp.var(h, axis=1, keepdims=True) + 1e-10
        return (h - mean) * scale * jax.lax.rsqrt(var) + offset
    h = jnp.maximum(_layernorm(x, axis=-1), 0.0)
    x = x + _L0_gnn_ref(h, src, dst, L0_gnn_theta_w, L0_gnn_theta_b, L0_gnn_phi_w, L0_gnn_phi_b)
    h = jnp.maximum(_layernorm(x, axis=-1), 0.0)
    x = x + _L1_gnn_ref(h, src, dst, edge_weight, L1_gnn_W1, L1_gnn_b1, L1_gnn_W2, L1_gnn_b2, L1_gnn_eps, L1_gnn_offset, L1_gnn_scale)
    return x

_drawn_inputs = setup_inputs


def setup_inputs(seed=0):
    import zlib

    import numpy as np

    out = dict(_drawn_inputs(seed))
    spreads = {'L0_gnn_theta_b': (0.0, 0.1),
     'L0_gnn_phi_b': (0.0, 0.1),
     'L1_gnn_b1': (0.0, 0.8),
     'L1_gnn_b2': (0.0, 0.735),
     'L1_gnn_offset': (0.0, 0.1),
     'L1_gnn_scale': (1.0, 0.2)}
    factors = {}
    for name, (base, spread) in spreads.items():
        noise = np.random.default_rng([zlib.crc32(name.encode()), seed]).standard_normal(out[name].shape)
        drawn = base * np.exp(spread * noise) if base else spread * noise
        out[name] = jnp.asarray(drawn.astype(out[name].dtype))
    for name, factor in factors.items():
        out[name] = (out[name] * factor).astype(out[name].dtype)
    return out
```

```python
import concourse.bass as bass
from concourse import mybir
from contextlib import ExitStack

F32 = mybir.dt.float32
I32 = mybir.dt.int32
BF16 = mybir.dt.bfloat16
ALU = mybir.AluOpType
ACT = mybir.ActivationFunctionType
AX = mybir.AxisListType

P = 128
HALF = 16
BATCH = 4
SLOTS = 4
ITER_STEPS = 2 * HALF
ITER_BATCHES = ITER_STEPS // BATCH
PEEL = 2
GROUP = 7
TABLES = BATCH
BIG = 3.0e38
LN_EPS = 1e-5
OUT_EPS = 1e-10


def two_gnn_layers(nc, x, src, dst, edge_weight, theta_w, theta_b, phi_w, phi_b,
                   w1, b1, w2, b2, eps, offset, scale, out):
    N, D = x.shape
    E = src.shape[0]
    KH = D // P
    NB = -(-N // P)
    NFULL, NREST = N // P, N % P
    CP = -(-E // (P * ITER_STEPS)) * ITER_STEPS
    ITERS = CP // ITER_STEPS
    NHALF = CP // HALF
    GROUPS = NB // GROUP
    PFULL, PREST = E // CP, E % CP
    PAD_DST = NB * P - 1
    assert D == 2 * P and NB == ITERS and NB % GROUP == 0 and 0 < NREST and N <= PAD_DST
    assert PFULL == P - 1 and 0 < PREST

    table_b = nc.dram_tensor("table_b", [NB * P, D], F32).ap()
    table_hw = nc.dram_tensor("table_hw", [NB * P, D], F32).ap()
    states = nc.dram_tensor("states", [P * CP + NB * P, D], F32).ap()
    edge_rows = states[0:P * CP, :].rearrange("(p k) d -> p k d", p=P)
    ROWS = NB * P + P
    sums = nc.dram_tensor("sums", [TABLES * ROWS, D], F32).ap()

    ctx = ExitStack()
    with ctx:
        def sb(name, shape, dt=F32):
            return ctx.enter_context(nc.sbuf_tensor(name, shape, dt))

        def sem(name):
            return ctx.enter_context(nc.semaphore(name))

        x_sb = sb("x_sb", [P, NB, D])
        a_sb = sb("a_sb", [P, NB, D])
        src_sb = sb("src_sb", [P, CP + P], I32)
        flags = sb("flags", [P, NHALF, 5, HALF])
        gring = sb("gring", [P, SLOTS * BATCH, D])
        sring = sb("sring", [P, SLOTS * BATCH, D])
        rows_n = sb("rows_n", [P, GROUP, D])
        dst_i = rows_n[:, :, :].rearrange("p a b -> p (a b)").bitcast(I32)[:, 0:CP]
        start_dst = sb("start_dst", [P, 1], I32)
        first_i = sb("first_i", [P, 1], I32)
        dst_f = gring[:, 0:8, :].rearrange("p a b -> p (a b)")[:, 0:CP + 1]
        dst_s = gring[:, 8:16, :].rearrange("p a b -> p (a b)").bitcast(I32)[:, 0:CP]
        w_f = sring[:, 8:16, :].rearrange("p a b -> p (a b)")[:, 0:CP]
        hst = sb("hst", [P, KH, D])
        idx_chunk = sb("idx_chunk", [P, 2, HALF], I32)
        flag_chunk = sb("flag_chunk", [P, 2, 3, HALF])
        pair_rows = sb("pair_rows", [P, 2 * BATCH * P])
        pairs = pair_rows[:, :].rearrange("p (a s q) -> p a s q", a=2, s=BATCH)
        onehot = pair_rows[:, :].bitcast(BF16)[:, 0:2 * BATCH * (P + NB)].rearrange(
            "p (a s q) -> p a s q", a=2, s=BATCH)
        last_chunk = sb("last_chunk", [P, GROUP], I32)
        ident = sb("ident", [P, P])
        upper = sb("upper", [P, P])
        ones = sb("ones", [P, P])
        iota_i = sb("iota_i", [P, P], I32)
        iota_f = sb("iota_f", [P, P])
        row_i = sb("row_i", [P, 1], I32)
        row_f = sb("row_f", [P, 1])
        w_nat = sring[:, 0:4, :].rearrange("p (m k) d -> p m k d", m=2)
        wb_t = sb("wb_t", [P, KH, D])
        wa_t = sb("wa_t", [P, KH, D])
        w1_sb = sb("w1_sb", [P, KH, D])
        w2_sb = sb("w2_sb", [P, KH, D])
        bias_a = sb("bias_a", [1, 2, D])
        b2_row = sb("b2_row", [1, D])
        b1_rows = sb("b1_rows", [P, D])
        off_rows = sb("off_rows", [P, D])
        scale_rows = sb("scale_rows", [P, D])
        eps1 = sb("eps1", [P, 1])
        ln = sb("ln", [P, NB, 2])
        bn = sb("bn", [P, GROUP, 6])
        mv = sb("mv", [P, GROUP, 2])
        std = sb("std", [P, GROUP])
        ln_eps = sb("ln_eps", [P, 2])
        zeros = sb("zeros", [P, P], BF16)
        cols = sb("cols", [P, 12])
        cont, whole, gate, gate_neg, cont_neg, nfirst = (cols[:, n:n + 1] for n in range(6))
        fix_f = cols[:, 6:7]
        fix_i = sb("fix_i", [P, 1], I32)
        gate_rows = sb("gate_rows", [P, P])
        carry_t = sb("carry_t", [P, KH, P + 1])
        hist = sb("hist", [P, NB])
        cum = sb("cum", [P, NB + 1])
        last_f = sb("last_f", [P, NB])
        last_i = sb("last_i", [P, NB], I32)
        has = sb("has", [P, NB])
        rows_in = gring[:, 0:GROUP, :]
        rows_t = gring[:, 7:7 + GROUP, :]
        rows_u = sring[:, 0:GROUP, :]
        rows_h = sring[:, 7:7 + GROUP, :]

        bank = [ctx.enter_context(nc.psum_tensor(f"bank{n}", [P, 512], F32)) for n in range(8)]
        hist_ps = bank[0][:, 0:NB]
        tp = [bank[1][:, 0:D], bank[2][:, 0:D]]
        mm = [bank[3][:, 0:D], bank[4][:, 0:D]]

        message = a_sb[:, 0:SLOTS * BATCH, :]
        block_sums = a_sb[:, 0:GROUP * TABLES, :].rearrange("p (b r) d -> p b r d", r=TABLES)
        flag_chunk1 = sb("flag_chunk1", [P, 2, 6, HALF])
        KEEP, WEIGHT, START, SRC, SPARE, TARGET = range(6)
        table_row = sb("table_row", [P, HALF])
        spare_f = sb("spare_f", [P, 1])
        before_me = sb("before_me", [P, P])
        twins = sb("twins", [P, 2, BATCH])
        shift = sb("shift", [P, BATCH])
        pair_waste = sb("pair_waste", [P, 2, BATCH, P], BF16)
        target = sb("target", [P, SLOTS, BATCH], I32)
        window = sb("window", [P, P])
        window_t = sb("window_t", [P, P])
        first_chunk = sb("first_chunk", [P, GROUP], I32)
        first_edge = sb("first_edge", [P, NB], I32)
        spare_edge = sb("spare_edge", [P, NB])
        node_i = sb("node_i", [P, NB], I32)
        src_rows = [bank[0], bank[3]]
        turned_ps = bank[0][:, 0:P]

        def combined(s):
            return bank[1 + s % 2][:, 0:D]

        def started(r, s):
            return bank[4 + 2 * r + s // 2][:, (s % 2) * D:(s % 2 + 1) * D]

        x0_loaded, x_loaded, theta_loaded = sem("x0_loaded"), sem("x_loaded"), sem("theta_loaded")
        edges_loaded, rows_loaded, mats_loaded = sem("edges_loaded"), sem("rows_loaded"), sem("mats_loaded")
        const_made, filled, iota_made = sem("const_made"), sem("filled"), sem("iota_made")
        pool_chain, dve_chain = sem("pool_chain"), sem("dve_chain")
        waited, dve_waited = sem("waited"), sem("dve_waited")
        wdiff_made, wt_turned, wt_ready = sem("wdiff_made"), sem("wt_turned"), sem("wt_ready")
        cols_ready = sem("cols_ready")
        p_stat, p_root, p_inverse, p_ln, p_norm = (sem(f"p_{n}") for n in ("stat", "root", "inverse", "ln", "norm"))
        p_turned, p_copied, p_product, p_evac = (sem(f"p_{n}") for n in ("turned", "copied", "product", "evac"))
        rows_stored = [sem(f"rows_stored{b}") for b in range(GROUP)]
        STORED = 16 * GROUPS
        gathered = [sem(f"gathered{r}") for r in range(SLOTS)]
        stored = [sem(f"stored{r}") for r in range(SLOTS)]
        idx_ready = sem("idx_ready")
        flag_ready = [sem(f"l{l}_flag_ready") for l in range(2)]
        folded = [sem(f"l{l}_folded") for l in range(2)]
        onehot_ready, onehot_used = sem("onehot_ready"), sem("onehot_used")
        s_norm, s_turned, s_copied, s_product, s_evac = (
            sem(f"side_{n}") for n in ("norm", "turned", "copied", "product", "evac"))
        side_done = sem("side_done")
        zeroed, zero_stored = sem("zeroed"), sem("zero_stored")
        start_gathered, start_ready, pairs_ready = sem("start_gathered"), sem("start_ready"), sem("pairs_ready")
        window_ready, window_turned, window_copied = sem("window_ready"), sem("window_turned"), sem("window_copied")
        src_spread, combined_ready, message_ready = sem("src_spread"), sem("combined_ready"), sem("message_ready")
        target_ready, table_free = sem("target_ready"), sem("table_free")
        message_read, shift_made = sem("message_read"), sem("shift_made")
        streamed = [sem(f"streamed{r}") for r in range(SLOTS)]
        scattered = [sem(f"scattered{r}") for r in range(TABLES)]
        hw_scattered = [sem(f"hw_scattered{b}") for b in range(GROUP)]
        own_made = sem("own_made")
        own_stored = [sem(f"own_stored{b}") for b in range(GROUP)]
        sums_loaded = [sem(f"sums_loaded{b}") for b in range(GROUP)]
        halved = sem("halved")
        zeros_made, hist_closed = sem("zeros_made"), sem("hist_closed")
        hist_copied, prefix_made, last_ready = sem("hist_copied"), sem("prefix_made"), sem("last_ready")
        gate_diag, gate_spread = sem("gate_diag"), sem("gate_spread")
        tail_turned = sem("tail_turned")
        carried = sem("carried")
        carry_turned = sem("carry_turned")
        fix_gathered = sem("fix_gathered")
        fix_made = sem("fix_made")
        fix_stored = sem("fix_stored")
        n_index = sem("n_index")
        n_gathered = [sem(f"n_gathered{b}") for b in range(GROUP)]
        n_comb, n_relu, n_x, n_stat, n_root, n_inverse, n_ln, n_norm, n_turned, n_copied, n_product, n_evac = (
            [sem(f"n{l}_{n}") for l in range(2)] for n in
            ("comb", "relu", "x", "stat", "root", "inverse", "ln", "norm", "turned", "copied", "product", "evac"))
        n_scaled, n_out = sem("n1_scaled"), sem("n1_out")

        block = ctx.enter_context(nc.Block())

        def over_blocks(eng, step, lag):
            for t in range(PEEL * GROUP):
                step(t, t % GROUP, t // GROUP)
            with eng.Fori(PEEL, GROUPS) as g:
                for b in range(GROUP):
                    step(g * GROUP + b, b, g)
            for t in range(NB, NB + lag):
                step(t, t % GROUP, t // GROUP)

        def uses(g, b, back):
            return g - 1 if b < back else g

        def live(t, back):
            return not isinstance(t, int) or 0 <= t - back < NB

        def later(t, n):
            return not isinstance(t, int) or t >= n

        def at(t, back):
            return t - back

        def blk(tile, t):
            if isinstance(t, int):
                return tile[:, t, :]
            return tile[:, bass.ds(t, 1), :].rearrange("p a d -> p (a d)")

        def col(tile, t, n=None):
            if n is None:
                return tile[:, t:t + 1] if isinstance(t, int) else tile[:, bass.ds(t, 1)]
            if isinstance(t, int):
                return tile[:, t, n:n + 1]
            return tile[:, bass.ds(t, 1), n:n + 1].rearrange("p a d -> p (a d)")

        @block.sync
        def _(sp):
            sp.wait_ge(filled, 1)
            x_blocks = x[0:NFULL * P, :].rearrange("(t p) d -> p t d", p=P)
            sp.dma_start(x_sb[:, 0:GROUP, :], x_blocks[:, 0:GROUP, :]).then_inc(x0_loaded, 16)
            sp.dma_start(w_nat[:, 0], theta_w.rearrange("(k p) d -> p k d", p=P)).then_inc(theta_loaded, 16)
            sp.dma_start(w_nat[:, 1], phi_w.rearrange("(k p) d -> p k d", p=P)).then_inc(theta_loaded, 16)
            for g in range(1, GROUPS):
                hi = min(g * GROUP + GROUP, NFULL)
                sp.dma_start(x_sb[:, g * GROUP:hi, :], x_blocks[:, g * GROUP:hi, :]).then_inc(x_loaded, 16)
            sp.dma_start(x_sb[0:NREST, NFULL, :], x[NFULL * P:N, :]).then_inc(x_loaded, 16)

            def store_b(t, b, g):
                sp.wait_ge(p_evac, t + 1)
                sp.dma_start(table_b[bass.ds(t * P, P), :], rows_n[:, b, :]).then_inc(rows_stored[b], 16)
            over_blocks(sp, store_b, 0)

            with sp.Fori(0, ITERS) as i:
                for b in range(ITER_BATCHES):
                    r = b % SLOTS
                    k = (i * ITER_BATCHES + b) * BATCH
                    sp.wait_ge(folded[0], k + BATCH)
                    sp.dma_start(edge_rows[:, bass.ds(k, BATCH), :],
                                 sring[:, r * BATCH:(r + 1) * BATCH, :]).then_inc(stored[r], 16)

            def store_hw(t, b, g):
                if live(t, 0):
                    sp.wait_ge(n_evac[0], t + 1)
                    sp.dma_start(table_hw[bass.ds(t * P, P), :], rows_n[:, b, :]).then_inc(rows_stored[b], 16)
                if live(t, 1):
                    u, c = at(t, 1), (b - 1) % GROUP
                    sp.wait_ge(own_made, u + 1)
                    sp.dma_start(sums[bass.ds(u * P, P), :], blk(a_sb, u)).then_inc(own_stored[c], 16)
            over_blocks(sp, store_hw, 1)

            for b in range(GROUP):
                sp.wait_ge(hw_scattered[b], 16 * GROUPS)

            def stream(i, first):
                for b in range(ITER_BATCHES):
                    r = b % SLOTS
                    n = i * ITER_BATCHES + b
                    if not first or b >= SLOTS:
                        sp.wait_ge(start_ready, n - SLOTS + 1)
                    sp.dma_start(gring[:, r * BATCH:(r + 1) * BATCH, :],
                                 edge_rows[:, bass.ds(n * BATCH, BATCH), :]).then_inc(streamed[r], 16)
            stream(0, True)
            with sp.Fori(1, ITERS) as i:
                stream(i, False)

            for r in range(TABLES):
                sp.wait_ge(scattered[r], 16 * CP // TABLES)
            tables = sums.rearrange("(r t p) d -> p r t d", r=TABLES, p=P)

            def load_sums(t, b, later_ones):
                if later_ones:
                    sp.wait_ge(n_comb[1], t - GROUP + 1)
                at_t = tables[:, :, t, :] if isinstance(t, int) else \
                    tables[:, :, bass.ds(t, 1), :].rearrange("p r a d -> p (r a) d")
                sp.dma_start(block_sums[:, b], at_t).then_inc(sums_loaded[b], 16)

            for b in range(GROUP):
                load_sums(b, b, False)

            def store_out(t, b, rows=P):
                sp.wait_ge(n_out, t + 1)
                sp.dma_start(out[bass.ds(t * P, rows), :], rows_h[0:rows, b, :]).then_inc(rows_stored[b], 16)
            with sp.Fori(0, GROUPS - 1) as g:
                for b in range(GROUP):
                    load_sums((g + 1) * GROUP + b, b, True)
                    store_out(g * GROUP + b, b)
            for t in range(NB - GROUP, NB):
                store_out(t, t % GROUP, P if t < NFULL else NREST)
            for b in range(GROUP):
                sp.wait_ge(rows_stored[b], 3 * STORED)

        @block.gpsimd
        def _(pool):
            chained = [0]

            def chain(instruction):
                chained[0] += 1
                instruction.then_inc(pool_chain, 1)
                pool.wait_ge(pool_chain, chained[0])

            pool.memset(x_sb[:, NFULL, :], 0.0).then_inc(filled, 1)
            pool.memset(dst_i[:, :], PAD_DST).then_inc(filled, 1)
            pool.memset(src_sb[:, :], 0).then_inc(filled, 1)
            pool.memset(w_f, 0.0).then_inc(filled, 1)
            pool.memset(first_i[:, :], -1).then_inc(filled, 1)
            pool.memset(ones[:, :], 1.0).then_inc(const_made, 1)
            chain(pool.memset(ident[:, :], 0.0))
            pool.affine_select(out=ident[:, :], in_=ident[:, :], compare_op=ALU.not_equal, fill=1.0,
                               base=0, pattern=[[-1, P]], channel_multiplier=1).then_inc(const_made, 1)
            chain(pool.memset(upper[:, :], 1.0))
            pool.affine_select(out=upper[:, :], in_=upper[:, :], compare_op=ALU.is_ge, fill=0.0,
                               base=0, pattern=[[1, P]], channel_multiplier=-1).then_inc(const_made, 1)
            pool.iota(iota_i[:, :], pattern=[[1, P]], base=0, channel_multiplier=0).then_inc(iota_made, 1)
            pool.iota(row_i[:, :], pattern=[[0, 1]], base=0, channel_multiplier=CP).then_inc(iota_made, 1)
            pool.iota(node_i[:, :], pattern=[[P, NB]], base=P * CP, channel_multiplier=1).then_inc(iota_made, 1)
            chain(pool.memset(before_me[:, :], 1.0))
            pool.affine_select(out=before_me[:, :], in_=before_me[:, :], compare_op=ALU.is_gt, fill=0.0,
                               base=0, pattern=[[-1, P]], channel_multiplier=1).then_inc(const_made, 1)
            for s in range(HALF):
                last = pool.memset(table_row[:, s:s + 1], float(s % TABLES * ROWS))
            last.then_inc(const_made, 1)
            pool.memset(a_sb[:, :, :], 0.0).then_inc(zeroed, 1)
            pool.wait_ge(zeroed, 1)
            for first_row, k in [(r * ROWS, NB) for r in range(1, TABLES)] + [(r * ROWS + NB * P, 1) for r in range(TABLES)]:
                pool.dma_start(sums[first_row:first_row + P * k, :].rearrange("(p k) d -> p (k d)", k=k),
                               a_sb[:, 0:k, :].rearrange("p k d -> p (k d)")).then_inc(zero_stored, 16)
            pool.dma_start(states[P * CP:P * CP + P * NB, :].rearrange("(p k) d -> p (k d)", k=NB),
                           a_sb[:, :, :].rearrange("p k d -> p (k d)")).then_inc(zero_stored, 16)

            def gather_edges(i, first):
                for b in range(ITER_BATCHES):
                    r, h = b % SLOTS, b * BATCH // HALF
                    if not first or b >= SLOTS:
                        pool.wait_ge(folded[0], (i * ITER_BATCHES + b - SLOTS + 1) * BATCH)
                    if b * BATCH % HALF == 0:
                        pool.wait_ge(idx_ready, 2 * i + h + 1)
                    pool.sem_inc(waited, 1)
                    for s in range(BATCH):
                        k = (b * BATCH + s) % HALF
                        pool.indirect_dma_start(
                            gring[:, r * BATCH + s, :], None, table_b,
                            bass.IndirectOffsetOnAxis(ap=idx_chunk[:, h, k:k + 1], axis=0)).then_inc(gathered[r], 16)
            for b in range(GROUP):
                pool.wait_ge(rows_stored[b], STORED)
            gather_edges(0, True)
            with pool.Fori(1, ITERS) as i:
                gather_edges(i, False)

            pool.wait_ge(cols_ready, 1)
            for r in range(SLOTS):
                pool.wait_ge(stored[r], 16 * CP // BATCH // SLOTS)
            pool.indirect_dma_start(rows_h[:, 0, :], None, states,
                                    bass.IndirectOffsetOnAxis(ap=fix_i[:, 0:1], axis=0)).then_inc(fix_gathered, 16)
            pool.wait_ge(fix_made, 1)
            pool.indirect_dma_start(states, bass.IndirectOffsetOnAxis(ap=fix_i[:, 0:1], axis=0),
                                    rows_h[:, 1, :], None).then_inc(fix_stored, 16)
            pool.wait_ge(fix_stored, 16)
            pool.wait_ge(zero_stored, 16 * 2 * TABLES)
            pool.wait_ge(last_ready, 1)

            def nodes0(t, b, g):
                if live(t, 0):
                    if later(t, GROUP):
                        pool.wait_ge(n_comb[0], t - GROUP + 1)
                    pool.tensor_copy(last_chunk[:, b:b + 1], col(last_i, t)).then_inc(n_index, 1)
                if live(t, 5):
                    u, c = at(t, 5), (b - 5) % GROUP
                    if later(u, GROUP):
                        pool.wait_ge(hw_scattered[c], 16 * uses(g, b, 5))
                    pool.tensor_copy(first_chunk[:, c:c + 1], col(first_edge, u)).then_inc(n_index, 1)
                    pool.wait_ge(n_evac[0], u + 1)
                pool.wait_ge(n_index, (t + 1 if live(t, 0) else NB) + (t - 4 if live(t, 5) else 0))
                pool.sem_inc(waited, 1)
                if live(t, 0):
                    pool.indirect_dma_start(rows_in[:, b, :], None, states,
                                            bass.IndirectOffsetOnAxis(ap=last_chunk[:, b:b + 1], axis=0))\
                        .then_inc(n_gathered[b], 16)
                if live(t, 5):
                    pool.indirect_dma_start(states, bass.IndirectOffsetOnAxis(ap=first_chunk[:, c:c + 1], axis=0),
                                            rows_n[:, c, :], None).then_inc(hw_scattered[c], 16)
            over_blocks(pool, nodes0, 5)

            for b in range(GROUP):
                pool.wait_ge(rows_stored[b], 2 * STORED)
            pool.indirect_dma_start(sring[:, SLOTS * BATCH - 1, :], None, table_hw,
                                    bass.IndirectOffsetOnAxis(ap=start_dst[:, :], axis=0)).then_inc(start_gathered, 16)
            for b in range(GROUP):
                pool.wait_ge(own_stored[b], 16 * GROUPS)

            def scatter_edges(i, first):
                for b in range(ITER_BATCHES):
                    n = i * ITER_BATCHES + b
                    pool.wait_ge(message_ready, n + 1)
                    pool.wait_ge(target_ready, n + 1)
                    for s in range(BATCH):
                        if not first or b > 0:
                            pool.wait_ge(scattered[s], 16 * n)
                        pool.sem_inc(table_free, 1)
                        pool.indirect_dma_start(
                            sums, bass.IndirectOffsetOnAxis(ap=target[:, b % SLOTS, s:s + 1], axis=0),
                            message[:, b % SLOTS * BATCH + s, :], None, compute_op=ALU.add).then_inc(scattered[s], 16)
            scatter_edges(0, True)
            with pool.Fori(1, ITERS) as i:
                scatter_edges(i, False)

            def nodes1(t, b, g):
                pool.wait_ge(sums_loaded[b], 16 * (g + 1))
                pool.tensor_tensor(block_sums[:, b, 0:2], block_sums[:, b, 0:2], block_sums[:, b, 2:4], ALU.add)\
                    .then_inc(halved, 1)
            over_blocks(pool, nodes1, 0)

        @block.scalar
        def _(act):
            act.wait_ge(filled, 5)
            for tile, array in ((dst_i, dst), (src_sb, src), (w_f, edge_weight)):
                act.dma_start(tile[0:PFULL, 0:CP], array[0:PFULL * CP].rearrange("(p k) -> p k", k=CP))\
                    .then_inc(edges_loaded, 16)
                act.dma_start(tile[PFULL:P, 0:PREST], array[PFULL * CP:E].rearrange("(p k) -> p k", p=1))\
                    .then_inc(edges_loaded, 16)
            with nc.allow_non_contiguous_dma(reason="one element per partition"):
                act.dma_start(first_i[1:P, :], dst[0:(P - 1) * CP].rearrange("(p k) -> p k", k=CP)[:, CP - 1:CP])\
                    .then_inc(edges_loaded, 16)
            for tile, array in ((b1_rows, b1), (off_rows, offset), (scale_rows, scale), (eps1, eps)):
                act.dma_start(tile[:, :], array.partition_broadcast(P)).then_inc(rows_loaded, 16)
            for tile, array in ((bias_a[:, 0, :], theta_b), (bias_a[:, 1, :], phi_b), (b2_row[:, :], b2)):
                act.dma_start(tile, array.rearrange("(a d) -> a d", a=1)).then_inc(rows_loaded, 16)
            act.dma_start(w1_sb[:, :, :], w1.rearrange("(k p) d -> p k d", p=P)).then_inc(mats_loaded, 16)
            act.dma_start(w2_sb[:, :, :], w2.rearrange("(k p) d -> p k d", p=P)).then_inc(mats_loaded, 16)

            def root(stat, done, t, b, layer):
                act.wait_ge(stat, 2 * t + 2)
                act.activation(std[:, b:b + 1], mv[:, b, 1:2], ACT.Sqrt, bias=ln_eps[:, layer:layer + 1]).then_inc(done, 1)

            def prelude(t, b, g):
                if live(t, 1):
                    u, c = at(t, 1), (b - 1) % GROUP
                    act.wait_ge(p_ln, u + 1)
                    if later(u, GROUP):
                        act.wait_ge(p_turned, u - GROUP + 1)
                    act.activation(rows_u[:, c, :], blk(x_sb, u), ACT.Relu, bias=col(ln, u, 1), scale=col(ln, u, 0))\
                        .then_inc(p_norm, 1)
                if live(t, 0):
                    root(p_stat, p_root, t, b, 0)
                if live(t, 3):
                    u, c = at(t, 3), (b - 3) % GROUP
                    act.wait_ge(p_product, u + 1)
                    if later(u, GROUP):
                        act.wait_ge(rows_stored[c], 16 * uses(g, b, 3))
                    act.activation(rows_n[:, c, :], mm[c % 2], ACT.Copy).then_inc(p_evac, 1)
            act.wait_ge(zeros_made, 3)
            act.wait_ge(wt_ready, 2)
            over_blocks(act, prelude, 3)

            act.wait_ge(zero_stored, 16 * 2 * TABLES)
            def iteration0(i, first):
                for h in range(2):
                    u = 2 * i + h
                    if not (first and h == 0):
                        act.wait_ge(folded[0], u * HALF)
                    act.activation(idx_chunk[:, 1 - h, :], src_sb[:, bass.ds((u + 1) * HALF, HALF)], ACT.Copy)\
                        .then_inc(idx_ready, 1)
                    if not first:
                        act.wait_ge(onehot_ready, (u - 1) * (HALF // BATCH))
                    f = flags[:, u, 0:3, :] if isinstance(u, int) else \
                        flags[:, bass.ds(u, 1), 0:3, :].rearrange("p a k s -> p (a k) s")
                    act.activation(flag_chunk[:, h], f, ACT.Copy).then_inc(flag_ready[0], 1)
                    if h == 0:
                        if not first:
                            act.wait_ge(s_turned, i)
                        act.activation(hst[:, 0, :], blk(x_sb, i), ACT.Relu, bias=col(ln, i, 1), scale=col(ln, i, 0))\
                            .then_inc(s_norm, 1)
                        act.wait_ge(s_turned, i + 1)
                        if not first:
                            act.wait_ge(s_product, i)
                        act.activation(hst[:, 1, :], tp[0], ACT.Copy).then_inc(s_copied, 1)
                    else:
                        act.wait_ge(s_product, i + 1)
                        act.activation(blk(a_sb, i), mm[0], ACT.Copy).then_inc(s_evac, 1)

            act.wait_ge(edges_loaded, 16 * 7)
            act.wait_ge(cols_ready, 1)
            act.activation(idx_chunk[:, 0, :], src_sb[:, 0:HALF], ACT.Copy).then_inc(idx_ready, 1)
            iteration0(0, True)
            with act.Fori(1, ITERS) as i:
                iteration0(i, False)

            def nodes0(t, b, g):
                if live(t, 0):
                    act.wait_ge(n_comb[0], t + 1)
                    act.activation(rows_u[:, b, :], rows_u[:, b, :], ACT.Relu, scale=col(has, t)).then_inc(n_relu[0], 1)
                if live(t, 2):
                    u, c = at(t, 2), (b - 2) % GROUP
                    act.wait_ge(n_ln[0], u + 1)
                    if later(u, GROUP):
                        act.wait_ge(n_turned[0], u - GROUP + 1)
                    act.activation(rows_h[:, c, :], blk(x_sb, u), ACT.Relu, bias=col(ln, u, 1), scale=col(ln, u, 0))\
                        .then_inc(n_norm[0], 1)
                if live(t, 1):
                    root(n_stat[0], n_root[0], at(t, 1), (b - 1) % GROUP, 0)
                if live(t, 3):
                    u, c = at(t, 3), (b - 3) % GROUP
                    act.wait_ge(n_turned[0], u + 1)
                    if later(u, GROUP):
                        act.wait_ge(n_product[0], u - GROUP + 1)
                    act.activation(rows_t[:, c, :], tp[c % 2], ACT.Copy).then_inc(n_copied[0], 1)
                if live(t, 4):
                    u, c = at(t, 4), (b - 4) % GROUP
                    act.wait_ge(n_product[0], u + 1)
                    if later(u, GROUP):
                        act.wait_ge(rows_stored[c], STORED + 16 * uses(g, b, 4))
                        act.wait_ge(hw_scattered[c], 16 * uses(g, b, 4))
                        act.wait_ge(own_made, u - GROUP + 1)
                    act.activation(rows_n[:, c, :], mm[c % 2], ACT.Copy).then_inc(n_evac[0], 1)
            act.wait_ge(fix_stored, 16)
            over_blocks(act, nodes0, 4)

            def stage1(u, h, first):
                if not first:
                    act.wait_ge(target_ready, (u - 1) * (HALF // BATCH))
                    act.wait_ge(pairs_ready, (u - 1) * (HALF // BATCH))
                f = flags[:, u, 3:5, :] if isinstance(u, int) else \
                    flags[:, bass.ds(u, 1), 3:5, :].rearrange("p a k s -> p (a k) s")
                k = flags[:, u, 3, :] if isinstance(u, int) else \
                    flags[:, bass.ds(u, 1), 3, :].rearrange("p a s -> p (a s)")
                now = src_sb[:, bass.ds(u * HALF, HALF)]
                act.activation(flag_chunk1[:, h, 0:2], f, ACT.Copy)
                act.activation(flag_chunk1[:, h, START], k, ACT.Copy, bias=1.0, scale=-1.0)
                act.activation(flag_chunk1[:, h, SRC], now, ACT.Copy)
                act.activation(flag_chunk1[:, h, SPARE], now, ACT.Identity, bias=spare_f[:, 0:1], scale=-1.0)\
                    .then_inc(flag_ready[1], 1)

            def messages(n, b, first):
                for s in range(BATCH):
                    act.wait_ge(combined_ready, n * BATCH + s + 1)
                    if s == 0 and not first:
                        act.wait_ge(table_free, (n - 2) * BATCH)
                    last = act.activation(message[:, b % SLOTS * BATCH + s, :], combined(s), ACT.Copy)
                    last.then_inc(message_read, 1)
                act.wait_ge(message_read, (n + 1) * BATCH)
                act.sem_inc(message_ready, 1)

            def window_in(i):
                act.activation(window[:, :], src_sb[:, bass.ds(i * ITER_STEPS, P)], ACT.Copy).then_inc(window_ready, 1)

            def window_out(i):
                act.wait_ge(window_turned, i + 1)
                act.activation(window_t[:, :], turned_ps, ACT.Copy).then_inc(window_copied, 1)

            def iteration1(i, first):
                for b in range(ITER_BATCHES):
                    n, h = i * ITER_BATCHES + b, b * BATCH // HALF
                    if b * BATCH % HALF == 0:
                        stage1(2 * i + h, h, first)
                        act.wait_ge(flag_ready[1], 2 * i + h + 1)
                    act.wait_ge(streamed[b % SLOTS], 16 * (2 * i + b // SLOTS + 1))
                    if not first or b >= 2:
                        act.wait_ge(folded[1], (n - 1) * BATCH)
                    for s in range(BATCH):
                        k = (b * BATCH + s) % HALF
                        last = act.activation(started(b % 2, s), gring[:, b % SLOTS * BATCH + s, :], ACT.Copy,
                                              scale=flag_chunk1[:, h, START, k:k + 1])
                    last.then_inc(start_ready, 1)
                    if not first or b > 0:
                        messages(n - 1, (b - 1) % SLOTS, first and b <= SLOTS)
                    if b == SLOTS:
                        window_in(i + 1)
                window_out(i + 1)
            act.wait_ge(own_made, NB)
            for b in range(GROUP):
                act.wait_ge(own_stored[b], 16 * GROUPS)
            window_in(0)
            window_out(0)
            iteration1(0, True)
            with act.Fori(1, ITERS) as i:
                iteration1(i, False)
            messages(CP // BATCH - 1, SLOTS - 1, False)

            def nodes1(t, b, g):
                if live(t, 0):
                    act.wait_ge(n_turned[1], t + 1)
                    if later(t, GROUP):
                        act.wait_ge(n_product[1], t - GROUP + 1)
                    act.activation(rows_t[:, b, :], tp[b % 2], ACT.Relu).then_inc(n_copied[1], 1)
                if live(t, 1):
                    u, c = at(t, 1), (b - 1) % GROUP
                    act.wait_ge(n_product[1], u + 1)
                    if later(u, GROUP):
                        act.wait_ge(n_scaled, u - GROUP + 1)
                    act.activation(rows_n[:, c, :], mm[c % 2], ACT.Relu).then_inc(n_evac[1], 1)
                if live(t, 2):
                    u, c = at(t, 2), (b - 2) % GROUP
                    act.wait_ge(n_ln[1], u + 1)
                    act.wait_ge(n_evac[1], u + 1)
                    act.activation(rows_n[:, c, :], rows_n[:, c, :], ACT.Identity, bias=col(ln, u, 1),
                                   scale=col(ln, u, 0)).then_inc(n_norm[1], 1)
                if live(t, 1):
                    root(n_stat[1], n_root[1], at(t, 1), (b - 1) % GROUP, 1)
            over_blocks(act, nodes1, 2)

        @block.tensor
        def _(pe):
            pe.wait_ge(const_made, 5)
            for m in range(2):
                pe.wait_ge(wdiff_made if m == 0 else theta_loaded, 1 if m == 0 else 32)
                if m == 1:
                    pe.wait_ge(wt_ready, 1)
                for k in range(KH):
                    for n in range(KH):
                        last = pe.transpose(tp[k][:, n * P:(n + 1) * P], w_nat[:, 1 - m, n, k * P:(k + 1) * P], ident[:, :])
                last.then_inc(wt_turned, 1)

            def turn(bank_ap, rows, done):
                for k in range(KH):
                    last = pe.transpose(bank_ap[:, k * P:(k + 1) * P], rows[:, k * P:(k + 1) * P], ident[:, :])
                last.then_inc(done, 1)

            def product(bank_ap, rows_turned, weights, done, bias=()):
                for k in range(KH):
                    last = pe.matmul(bank_ap, rows_turned[:, k * P:(k + 1) * P], weights[:, k, :],
                                     start=(k == 0), stop=(k == KH - 1 and not bias))
                for n, row in enumerate(bias):
                    last = pe.matmul(bank_ap, ones[0:1, :], row, start=False, stop=(n == len(bias) - 1))
                last.then_inc(done, 1)

            pe.wait_ge(wt_ready, 2)

            def prelude(t, b, g):
                if live(t, 1):
                    u, c = at(t, 1), (b - 1) % GROUP
                    pe.wait_ge(p_norm, u + 1)
                    if later(u, 1 if c == 0 else 2):
                        pe.wait_ge(p_copied, u if c == 0 else u - 1)
                    turn(tp[c % 2], rows_u[:, c, :], p_turned)
                if live(t, 2):
                    u, c = at(t, 2), (b - 2) % GROUP
                    pe.wait_ge(p_copied, u + 1)
                    if later(u, 1 if c == 0 else 2):
                        pe.wait_ge(p_evac, u if c == 0 else u - 1)
                    product(mm[c % 2], rows_t[:, c, :], wb_t, p_product)
            over_blocks(pe, prelude, 2)

            def iteration0(i, first):
                pe.wait_ge(s_norm, i + 1)
                if not first:
                    pe.wait_ge(s_copied, i)
                else:
                    pe.wait_ge(p_copied, NB)
                turn(tp[0], hst[:, 0, :], s_turned)
                for b in range(ITER_BATCHES):
                    pe.wait_ge(onehot_ready, i * ITER_BATCHES + b + 1)
                    for s in range(BATCH):
                        last = pe.matmul(hist_ps, onehot[:, b % 2, s, 0:P], onehot[:, b % 2, s, P:P + NB],
                                         start=(first and b == 0 and s == 0), stop=False)
                    last.then_inc(onehot_used, 1)
                    if b == 2:
                        pe.wait_ge(s_copied, i + 1)
                        if not first:
                            pe.wait_ge(s_evac, i)
                        else:
                            pe.wait_ge(p_evac, NB)
                        product(mm[0], hst[:, 1, :], wa_t, s_product, (bias_a[:, 0, :], bias_a[:, 1, :]))
            pe.wait_ge(rows_loaded, 16 * 7)
            iteration0(0, True)
            with pe.Fori(1, ITERS) as i:
                iteration0(i, False)
            pe.wait_ge(zeros_made, 1)
            pe.matmul(hist_ps, zeros[:, :], zeros[:, 0:NB], start=False, stop=True).then_inc(hist_closed, 1)

            pe.wait_ge(hist_copied, 1)
            pe.matmul(bank[4][:, 0:NB], upper[:, :], hist[:, :], start=True, stop=True)
            pe.matmul(bank[4][:, 64:64 + NB], ones[:, :], hist[:, :], start=True, stop=True).then_inc(prefix_made, 1)
            pe.wait_ge(gate_diag, 1)
            pe.matmul(bank[5][:, 0:P], ones[:, :], hst[:, 0, 0:P], start=True, stop=True).then_inc(gate_spread, 1)

            pe.wait_ge(s_evac, ITERS)
            pe.wait_ge(folded[0], CP)
            turn(tp[0], sring[:, SLOTS * BATCH - 1, :], tail_turned)
            pe.wait_ge(carried, 1)
            for k in range(KH):
                last = pe.transpose(mm[0][:, k * P:(k + 1) * P], carry_t[:, k, 0:P], ident[:, :])
            last.then_inc(carry_turned, 1)
            pe.wait_ge(fix_made, 1)

            def nodes0(t, b, g):
                if live(t, 2):
                    u, c = at(t, 2), (b - 2) % GROUP
                    pe.wait_ge(n_norm[0], u + 1)
                    if later(u, 1 if c == 0 else 2):
                        pe.wait_ge(n_copied[0], u if c == 0 else u - 1)
                    turn(tp[c % 2], rows_h[:, c, :], n_turned[0])
                if live(t, 3):
                    u, c = at(t, 3), (b - 3) % GROUP
                    pe.wait_ge(n_copied[0], u + 1)
                    if later(u, 1 if c == 0 else 2):
                        pe.wait_ge(n_evac[0], u if c == 0 else u - 1)
                    product(mm[c % 2], rows_t[:, c, :], w1_sb, n_product[0])
            pe.wait_ge(mats_loaded, 32)
            over_blocks(pe, nodes0, 3)

            def turn_window(i):
                pe.wait_ge(window_ready, i + 1)
                pe.transpose(turned_ps, window[:, :], ident[:, :]).then_inc(window_turned, 1)
                pe.wait_ge(window_copied, i + 1)

            def spread(n, b):
                for s in range(BATCH):
                    k = b * BATCH + s
                    last = pe.matmul(src_rows[b % 2][:, s * P:(s + 1) * P], ident[:, k:k + 1].to_broadcast([P, P]),
                                     window_t[:, :], start=True, stop=True)
                last.then_inc(src_spread, 1)

            def iteration1(i, first):
                for b in range(ITER_BATCHES):
                    n = i * ITER_BATCHES + b
                    if not (first and b == 0):
                        pe.wait_ge(pairs_ready, n)
                    if b == ITER_BATCHES - 1:
                        turn_window(i + 1)
                    spread(n + 1, (b + 1) % ITER_BATCHES)
                    pe.wait_ge(pairs_ready, n + 1)
                    pe.wait_ge(folded[1], (n + 1) * BATCH)
                    for s in range(BATCH):
                        if not (first and b == 0 and s < 2):
                            pe.wait_ge(message_read, n * BATCH + s - 1)
                        pe.matmul(combined(s), pairs[:, b % 2, s, :], sring[:, b % SLOTS * BATCH + s, :],
                                  start=True, stop=True).then_inc(combined_ready, 1)
            pe.wait_ge(n_evac[0], NB)
            turn_window(0)
            spread(0, 0)
            iteration1(0, True)
            with pe.Fori(1, ITERS) as i:
                iteration1(i, False)
            pe.wait_ge(message_read, CP)

            def nodes1(t, b, g):
                if live(t, 0):
                    pe.wait_ge(n_comb[1], t + 1)
                    if later(t, 1 if b == 0 else 2):
                        pe.wait_ge(n_copied[1], t if b == 0 else t - 1)
                    turn(tp[b % 2], rows_u[:, b, :], n_turned[1])
                if live(t, 1):
                    u, c = at(t, 1), (b - 1) % GROUP
                    pe.wait_ge(n_copied[1], u + 1)
                    if later(u, 1 if c == 0 else 2):
                        pe.wait_ge(n_evac[1], u if c == 0 else u - 1)
                    product(mm[c % 2], rows_t[:, c, :], w2_sb, n_product[1], (b2_row[:, :],))
            over_blocks(pe, nodes1, 1)

        @block.vector
        def _(dve):
            chained = [0]

            def chain(instruction):
                chained[0] += 1
                instruction.then_inc(dve_chain, 1)
                dve.wait_ge(dve_chain, chained[0])

            dve.memset(zeros[:, :], 0.0).then_inc(zeros_made, 1)
            dve.memset(ln_eps[:, 0:1], LN_EPS).then_inc(zeros_made, 1)
            dve.memset(ln_eps[:, 1:2], OUT_EPS).then_inc(zeros_made, 1)
            dve.wait_ge(theta_loaded, 32)
            dve.tensor_tensor(w_nat[:, 1], w_nat[:, 1], w_nat[:, 0], ALU.subtract).then_inc(wdiff_made, 1)
            for m, tile in enumerate((wb_t, wa_t)):
                dve.wait_ge(wt_turned, m + 1)
                for k in range(KH):
                    last = dve.tensor_copy(tile[:, k, :], tp[k])
                last.then_inc(wt_ready, 1)

            dve.wait_ge(edges_loaded, 16 * 7)
            dve.wait_ge(iota_made, 3)
            chain(dve.tensor_copy(iota_f[:, :], iota_i[:, :]))
            chain(dve.tensor_copy(row_f[:, :], row_i[:, :]))
            dve.tensor_copy(dst_f[:, 0:1], first_i[:, :])
            dve.tensor_copy(start_dst[:, :], dst_i[:, 0:1])
            chain(dve.tensor_copy(dst_f[:, 1:CP + 1], dst_i[:, :]))
            now = dst_f[:, 1:CP + 1].rearrange("p (h s) -> p h s", s=HALF)
            before = dst_f[:, 0:CP].rearrange("p (h s) -> p h s", s=HALF)
            chain(dve.tensor_tensor(flags[:, :, 3, :], now, before, ALU.is_equal))
            chain(dve.tensor_copy(cont, flags[:, 0, 3, 0:1]))
            chain(dve.memset(flags[:, 0, 3, 0:1], 0.0))
            chain(dve.tensor_scalar(flags[:, :, 0, :], flags[:, :, 3, :], -1.0, BIG, ALU.add, ALU.mult))
            dve.memset(flags[:, 0, 3, 0:1], 1.0)
            dve.tensor_copy(spare_edge[:, :], node_i[:, :])
            chain(dve.tensor_copy(spare_f[:, :], node_i[:, 0:1]))
            chain(dve.tensor_scalar(spare_f[:, :], spare_f[:, :], float(NB * P - P * CP), None, ALU.add))
            dve.tensor_copy(flags[:, :, 4, :], w_f.rearrange("p (h s) -> p h s", s=HALF))
            halves = dst_s.rearrange("p (h s) -> p h s", s=HALF)
            chain(dve.tensor_scalar(dst_s, dst_i[:, :], 7, None, ALU.arith_shift_right))
            chain(dve.tensor_copy(flags[:, :, 1, :], halves))
            chain(dve.tensor_scalar(dst_s, dst_i[:, :], P - 1, None, ALU.bitwise_and))
            chain(dve.tensor_copy(flags[:, :, 2, :], halves))
            same = dst_s.bitcast(F32)
            chain(dve.tensor_scalar(same, dst_f[:, 1:CP + 1], dst_f[:, 1:2], None, ALU.is_equal))
            chain(dve.tensor_reduce(nfirst, same, AX.X, ALU.add))
            chain(dve.tensor_copy(whole, same[:, CP - 1:CP]))
            chain(dve.tensor_tensor(gate, cont, whole, ALU.mult))
            dve.tensor_scalar(gate_neg, gate, -1.0, BIG, ALU.add, ALU.mult)
            dve.tensor_scalar(cont_neg, cont, -1.0, BIG, ALU.add, ALU.mult)
            chain(dve.scalar_tensor_tensor(fix_f, nfirst, -1.0, row_f[:, :], ALU.add, ALU.add))
            dve.tensor_copy(fix_i[:, :], fix_f).then_inc(cols_ready, 1)

            def statistics(rows, stat, t, b):
                dve.sem_inc(dve_waited, 1)
                dve.bn_stats(bn[:, b, :], rows).then_inc(stat, 1)
                dve.wait_ge(stat, 2 * t + 1)
                dve.sem_inc(dve_waited, 1)
                dve.bn_aggr(mv[:, b, :], bn[:, b, :]).then_inc(stat, 1)

            def factors(root, inverse, done, t, b):
                dve.wait_ge(root, t + 1)
                dve.reciprocal(col(ln, t, 0), std[:, b:b + 1]).then_inc(inverse, 1)
                dve.wait_ge(inverse, t + 1)
                dve.scalar_tensor_tensor(col(ln, t, 1), mv[:, b, 0:1], -1.0, col(ln, t, 0), ALU.mult, ALU.mult)\
                    .then_inc(done, 1)

            def prelude(t, b, g):
                if live(t, 1):
                    factors(p_root, p_inverse, p_ln, at(t, 1), (b - 1) % GROUP)
                if live(t, 0):
                    if isinstance(t, int):
                        if t in (0, GROUP):
                            dve.wait_ge(x_loaded if t else x0_loaded, 16 * GROUPS if t else 16)
                    statistics(blk(x_sb, t), p_stat, t, b)
                if live(t, 2):
                    u, c = at(t, 2), (b - 2) % GROUP
                    dve.wait_ge(p_turned, u + 1)
                    if later(u, GROUP):
                        dve.wait_ge(p_product, u - GROUP + 1)
                    dve.tensor_copy(rows_t[:, c, :], tp[c % 2]).then_inc(p_copied, 1)
            over_blocks(dve, prelude, 2)

            def iteration0(i, first):
                for b in range(ITER_BATCHES):
                    r, h = b % SLOTS, b * BATCH // HALF
                    n = i * ITER_BATCHES + b
                    if b * BATCH % HALF == 0:
                        dve.wait_ge(flag_ready[0], 2 * i + h + 1)
                    if not first or b >= 2:
                        dve.wait_ge(onehot_used, n - 1)
                    if not first or b >= SLOTS:
                        dve.wait_ge(stored[r], 16 * (2 * i + b // SLOTS))
                    dve.wait_ge(gathered[r], 16 * BATCH * (2 * i + b // SLOTS + 1))
                    for s in range(BATCH):
                        k = (b * BATCH + s) % HALF
                        if not (first and b == 0 and s == 0):
                            dve.wait_ge(folded[0], n * BATCH + s)
                        dve.scalar_tensor_tensor(sring[:, r * BATCH + s, :], sring[:, (r * BATCH + s - 1) % (SLOTS * BATCH), :],
                                                 flag_chunk[:, h, 0, k:k + 1], gring[:, r * BATCH + s, :],
                                                 ALU.add, ALU.max).then_inc(folded[0], 1)
                        dve.tensor_scalar(onehot[:, b % 2, s, 0:P], iota_f[:, :], flag_chunk[:, h, 2, k:k + 1],
                                          None, ALU.is_equal)
                        last = dve.tensor_scalar(onehot[:, b % 2, s, P:P + NB], iota_f[:, 0:NB],
                                                 flag_chunk[:, h, 1, k:k + 1], None, ALU.is_equal)
                    last.then_inc(onehot_ready, 1)
            for b in range(GROUP):
                dve.wait_ge(rows_stored[b], STORED)
            chain(dve.memset(sring[:, SLOTS * BATCH - 1, :], 0.0))
            iteration0(0, True)
            with dve.Fori(1, ITERS) as i:
                iteration0(i, False)

            dve.wait_ge(hist_closed, 1)
            chain(dve.tensor_copy(hist[:, :], hist_ps))
            dve.tensor_scalar(has[:, :], hist[:, :], 0.0, None, ALU.is_gt).then_inc(hist_copied, 1)
            chain(dve.memset(cum[:, 0:1], -1.0))
            dve.wait_ge(hist_copied, 1)
            dve.wait_ge(prefix_made, 1)
            one_row = ones[:, 0:NB]
            chain(dve.tensor_tensor_scan(cum[:, 1:NB + 1], one_row, bank[4][:, 64:64 + NB], -1.0, ALU.mult, ALU.add))
            chain(dve.tensor_tensor(last_f[:, :], bank[4][:, 0:NB], cum[:, 0:NB], ALU.add))
            chain(dve.tensor_tensor(last_f[:, :], last_f[:, :], spare_edge[:, :], ALU.subtract))
            chain(dve.scalar_tensor_tensor(hist[:, :], hist[:, :], -1.0, last_f[:, :], ALU.mult, ALU.add))
            chain(dve.tensor_tensor(last_f[:, :], last_f[:, :], has[:, :], ALU.mult))
            chain(dve.scalar_tensor_tensor(hist[:, :], hist[:, :], 1.0, has[:, :], ALU.add, ALU.mult))
            chain(dve.tensor_tensor(last_i[:, :], last_f[:, :], spare_edge[:, :], ALU.add))
            dve.tensor_tensor(first_edge[:, :], hist[:, :], spare_edge[:, :], ALU.add).then_inc(last_ready, 1)
            dve.wait_ge(s_copied, ITERS)
            dve.tensor_scalar(hst[:, 0, 0:P], ident[:, :], gate, None, ALU.mult).then_inc(gate_diag, 1)
            dve.wait_ge(gate_spread, 1)
            chain(dve.tensor_scalar(gate_rows[:, :], bank[5][:, 0:P], -1.0, BIG, ALU.add, ALU.mult))

            dve.memset(carry_t[:, :, 0:1], 0.0)
            dve.wait_ge(tail_turned, 1)
            for k in range(KH):
                last = dve.tensor_tensor_scan(carry_t[:, k, 1:P + 1], gate_rows[:, :],
                                              tp[0][:, k * P:(k + 1) * P], 0.0, ALU.add, ALU.max)
            last.then_inc(carried, 1)
            dve.wait_ge(carry_turned, 1)
            dve.wait_ge(fix_gathered, 16)
            dve.scalar_tensor_tensor(rows_h[:, 1, :], mm[0], cont_neg, rows_h[:, 0, :], ALU.add, ALU.max)\
                .then_inc(fix_made, 1)

            def nodes0(t, b, g):
                if live(t, 0):
                    dve.wait_ge(n_gathered[b], 16 * (g + 1))
                    if later(t, GROUP):
                        dve.wait_ge(n_x[0], t - GROUP + 1)
                    dve.tensor_tensor(rows_u[:, b, :], rows_in[:, b, :], blk(a_sb, t), ALU.add).then_inc(n_comb[0], 1)
                if live(t, 2):
                    factors(n_root[0], n_inverse[0], n_ln[0], at(t, 2), (b - 2) % GROUP)
                if live(t, 1):
                    u, c = at(t, 1), (b - 1) % GROUP
                    dve.wait_ge(n_relu[0], u + 1)
                    dve.tensor_tensor(blk(x_sb, u), blk(x_sb, u), rows_u[:, c, :], ALU.add).then_inc(n_x[0], 1)
                    dve.wait_ge(n_x[0], u + 1)
                    statistics(blk(x_sb, u), n_stat[0], u, c)
                if live(t, 5):
                    u, c = at(t, 5), (b - 5) % GROUP
                    dve.wait_ge(n_evac[0], u + 1)
                    dve.scalar_tensor_tensor(blk(a_sb, u), rows_n[:, c, :], eps1[:, 0:1], b1_rows[:, :],
                                             ALU.mult, ALU.add).then_inc(own_made, 1)
            dve.wait_ge(s_evac, ITERS)
            dve.wait_ge(rows_loaded, 16 * 7)
            chain(dve.tensor_scalar(eps1[:, :], eps1[:, :], 1.0, None, ALU.add))
            over_blocks(dve, nodes0, 5)

            def iteration1(i, first):
                for b in range(ITER_BATCHES):
                    r, h = b % SLOTS, b * BATCH // HALF
                    n = i * ITER_BATCHES + b
                    if b * BATCH % HALF == 0:
                        dve.wait_ge(flag_ready[1], 2 * i + h + 1)
                        dve.tensor_tensor(flag_chunk1[:, h, TARGET], flag_chunk1[:, h, SRC], table_row[:, :], ALU.add)
                    if not first or b >= 2:
                        dve.wait_ge(combined_ready, (n - 1) * BATCH)
                    dve.wait_ge(start_ready, n + 1)
                    dve.wait_ge(src_spread, n + 1)
                    for s in range(BATCH):
                        k = (b * BATCH + s) % HALF
                        if not (first and b == 0 and s == 0):
                            dve.wait_ge(folded[1], n * BATCH + s)
                        dve.scalar_tensor_tensor(sring[:, r * BATCH + s, :], sring[:, (r * BATCH + s - 1) % (SLOTS * BATCH), :],
                                                 flag_chunk1[:, h, KEEP, k:k + 1], started(b % 2, s),
                                                 ALU.mult, ALU.add).then_inc(folded[1], 1)
                        sources = src_rows[b % 2][:, s * P:(s + 1) * P]
                        dve.tensor_scalar(pairs[:, b % 2, s, :], sources, flag_chunk1[:, h, SRC, k:k + 1],
                                          flag_chunk1[:, h, WEIGHT, k:k + 1], ALU.is_equal, ALU.mult)
                        last = dve.scalar_tensor_tensor(pair_waste[:, b % 2, s], sources, flag_chunk1[:, h, SRC, k:k + 1],
                                                        before_me[:, :], ALU.is_equal, ALU.mult,
                                                        accum_out=twins[:, b % 2, s:s + 1])
                    last.then_inc(pairs_ready, 1)
                    dve.wait_ge(pairs_ready, n + 1)
                    k = b * BATCH % HALF
                    dve.scalar_tensor_tensor(shift[:, :], twins[:, b % 2, :], 0.0, flag_chunk1[:, h, SPARE, k:k + BATCH],
                                             ALU.is_gt, ALU.mult).then_inc(shift_made, 1)
                    dve.wait_ge(shift_made, n + 1)
                    if not first or b >= SLOTS:
                        dve.wait_ge(table_free, (n - 2) * BATCH)
                    dve.tensor_tensor(target[:, r, :], shift[:, :], flag_chunk1[:, h, TARGET, k:k + BATCH], ALU.add)\
                        .then_inc(target_ready, 1)
                    if b == 4:
                        dve.tensor_tensor(blk(x_sb, i), blk(x_sb, i), off_rows[:, :], ALU.add).then_inc(side_done, 1)
            dve.wait_ge(start_gathered, 16)
            iteration1(0, True)
            with dve.Fori(1, ITERS) as i:
                iteration1(i, False)
            dve.wait_ge(side_done, ITERS)

            def nodes1(t, b, g):
                if live(t, 0):
                    dve.wait_ge(halved, t + 1)
                    if later(t, GROUP):
                        dve.wait_ge(n_turned[1], t - GROUP + 1)
                    dve.tensor_tensor(rows_u[:, b, :], block_sums[:, b, 0], block_sums[:, b, 1], ALU.add)\
                        .then_inc(n_comb[1], 1)
                if live(t, 2):
                    factors(n_root[1], n_inverse[1], n_ln[1], at(t, 2), (b - 2) % GROUP)
                if live(t, 1):
                    u, c = at(t, 1), (b - 1) % GROUP
                    dve.wait_ge(n_evac[1], u + 1)
                    statistics(rows_n[:, c, :], n_stat[1], u, c)
                if live(t, 3):
                    u, c = at(t, 3), (b - 3) % GROUP
                    dve.wait_ge(n_norm[1], u + 1)
                    if later(u, GROUP):
                        dve.wait_ge(rows_stored[c], 2 * STORED + 16 * uses(g, b, 3))
                    dve.tensor_tensor(rows_h[:, c, :], rows_n[:, c, :], scale_rows[:, :], ALU.mult).then_inc(n_scaled, 1)
                    dve.wait_ge(n_scaled, u + 1)
                    dve.tensor_tensor(rows_h[:, c, :], rows_h[:, c, :], blk(x_sb, u), ALU.add).then_inc(n_out, 1)
            over_blocks(dve, nodes1, 3)


_INS = ['x', 'src', 'dst', 'edge_weight', 'L0_gnn_theta_w', 'L0_gnn_theta_b', 'L0_gnn_phi_w', 'L0_gnn_phi_b',
        'L1_gnn_W1', 'L1_gnn_b1', 'L1_gnn_W2', 'L1_gnn_b2', 'L1_gnn_eps', 'L1_gnn_offset', 'L1_gnn_scale']


def kernel(**inputs):
    import numpy as _np
    import concourse.bacc as _bacc
    from concourse import mybir as _mybir
    from concourse.bass_utils import run_bass_kernel_spmd as _run

    nc = _bacc.Bacc("TRN2", target_bir_lowering=False, num_devices=1)
    arrays, args = {}, []
    for name in _INS:
        a = _np.ascontiguousarray(inputs[name])
        arrays[f"in_{name}"] = a
        args.append(nc.dram_tensor(f"in_{name}", a.shape, _mybir.dt.from_np(a.dtype), kind="ExternalInput").ap())
    out = nc.dram_tensor("out_x", inputs['x'].shape, _mybir.dt.float32, kind="ExternalOutput").ap()
    two_gnn_layers(nc, *args, out)
    r = _run(nc, [arrays], core_ids=[0])
    return r.results[0]["out_x"]
```

```python
import concourse.bass as bass
from concourse import mybir
from contextlib import ExitStack

F32 = mybir.dt.float32
I32 = mybir.dt.int32
BF16 = mybir.dt.bfloat16
ALU = mybir.AluOpType
ACT = mybir.ActivationFunctionType
AX = mybir.AxisListType

P = 128
HALF = 16
BATCH = 4
SLOTS = 4
ITER_STEPS = 2 * HALF
ITER_BATCHES = ITER_STEPS // BATCH
PEEL = 2
GROUP = 7
TABLES = BATCH
BIG = 3.0e38
LN_EPS = 1e-5
OUT_EPS = 1e-10


def two_gnn_layers(nc, x, src, dst, edge_weight, theta_w, theta_b, phi_w, phi_b,
                   w1, b1, w2, b2, eps, offset, scale, out):
    N, D = x.shape
    E = src.shape[0]
    KH = D // P
    NB = -(-N // P)
    NFULL, NREST = N // P, N % P
    CP = -(-E // (P * ITER_STEPS)) * ITER_STEPS
    ITERS = CP // ITER_STEPS
    NHALF = CP // HALF
    GROUPS = NB // GROUP
    PFULL, PREST = E // CP, E % CP
    PAD_DST = NB * P - 1
    assert D == 2 * P and NB == ITERS and NB % GROUP == 0 and 0 < NREST and N <= PAD_DST
    assert PFULL == P - 1 and 0 < PREST

    table_b = nc.dram_tensor("table_b", [NB * P, D], F32).ap()
    table_hw = nc.dram_tensor("table_hw", [NB * P, D], F32).ap()
    states = nc.dram_tensor("states", [P * CP + NB * P, D], F32).ap()
    edge_rows = states[0:P * CP, :].rearrange("(p k) d -> p k d", p=P)
    ROWS = NB * P + P
    sums = nc.dram_tensor("sums", [TABLES * ROWS, D], F32).ap()

    ctx = ExitStack()
    with ctx:
        def sb(name, shape, dt=F32):
            return ctx.enter_context(nc.sbuf_tensor(name, shape, dt))

        def sem(name):
            return ctx.enter_context(nc.semaphore(name))

        x_sb = sb("x_sb", [P, NB, D])
        a_sb = sb("a_sb", [P, NB, D])
        src_sb = sb("src_sb", [P, CP + P], I32)
        flags = sb("flags", [P, NHALF, 5, HALF])
        gring = sb("gring", [P, SLOTS * BATCH, D])
        sring = sb("sring", [P, SLOTS * BATCH, D])
        rows_n = sb("rows_n", [P, GROUP, D])

        def edge_array(n):
            w = -(-(CP + 1) // D)
            return a_sb[:, n * w:(n + 1) * w, :].rearrange("p a b -> p (a b)")
        dst_i = edge_array(0).bitcast(I32)[:, 0:CP]
        start_dst = sb("start_dst", [P, 1], I32)
        first_i = sb("first_i", [P, 1], I32)
        zero_rows = rows_n[:, 0:TABLES, :]
        dst_f = edge_array(1)[:, 0:CP + 1]
        dst_s = edge_array(2).bitcast(I32)[:, 0:CP]
        w_f = edge_array(3)[:, 0:CP]
        hst = sb("hst", [P, KH, D])
        idx_chunk = sb("idx_chunk", [P, 2, HALF], I32)
        flag_chunk = sb("flag_chunk", [P, 2, 3, HALF])
        pair_rows = sb("pair_rows", [P, 2 * BATCH * P])
        pairs = pair_rows[:, :].rearrange("p (a s q) -> p a s q", a=2, s=BATCH)
        onehot = pair_rows[:, :].bitcast(BF16)[:, 0:2 * BATCH * (P + NB)].rearrange(
            "p (a s q) -> p a s q", a=2, s=BATCH)
        last_chunk = sb("last_chunk", [P, GROUP], I32)
        ident = sb("ident", [P, P])
        upper = sb("upper", [P, P])
        ones = sb("ones", [P, P])
        iota_i = sb("iota_i", [P, P], I32)
        iota_f = sb("iota_f", [P, P])
        row_i = sb("row_i", [P, 1], I32)
        row_f = sb("row_f", [P, 1])
        w_nat = sring[:, 0:4, :].rearrange("p (m k) d -> p m k d", m=2)
        wb_t = sb("wb_t", [P, KH, D])
        wa_t = sb("wa_t", [P, KH, D])
        w1_sb = sb("w1_sb", [P, KH, D])
        w2_sb = sb("w2_sb", [P, KH, D])
        bias_a = sb("bias_a", [1, 2, D])
        b2_row = sb("b2_row", [1, D])
        b1_rows = sb("b1_rows", [P, D])
        off_rows = sb("off_rows", [P, D])
        scale_rows = sb("scale_rows", [P, D])
        eps1 = sb("eps1", [P, 1])
        ln = sb("ln", [P, NB, 2])
        bn = sb("bn", [P, GROUP, 6])
        mv = sb("mv", [P, GROUP, 2])
        std = sb("std", [P, GROUP])
        ln_eps = sb("ln_eps", [P, 2])
        zeros = sb("zeros", [P, P], BF16)
        cols = sb("cols", [P, 6])
        cont, whole, gate, cont_neg, nfirst, fix_f = (cols[:, n:n + 1] for n in range(6))
        fix_i = sb("fix_i", [P, 1], I32)
        gate_rows = sb("gate_rows", [P, P])
        carry_t = sb("carry_t", [P, KH, P + 1])
        hist = sb("hist", [P, NB])
        cum = sb("cum", [P, NB + 1])
        last_f = sb("last_f", [P, NB])
        last_i = sb("last_i", [P, NB + GROUP], I32)
        has = sb("has", [P, NB])
        rows_in = gring[:, 0:GROUP, :]
        rows_t = gring[:, GROUP:2 * GROUP, :]
        rows_u = sring[:, 0:GROUP, :]
        rows_h = sring[:, GROUP:2 * GROUP, :]

        bank = [ctx.enter_context(nc.psum_tensor(f"bank{n}", [P, 512], F32)) for n in range(8)]
        hist_ps = bank[0][:, 0:NB]
        tp = [bank[1][:, 0:D], bank[2][:, 0:D]]
        mm = [bank[3][:, 0:D], bank[4][:, 0:D]]

        message = a_sb[:, 0:SLOTS * BATCH, :]
        sources = a_sb[:, SLOTS * BATCH:SLOTS * BATCH + 4, :].rearrange("p (a s) (t q) -> p a (s t) q", a=2, q=P)
        block_sums = a_sb[:, 0:GROUP * TABLES, :].rearrange("p (b r) d -> p b r d", r=TABLES)
        flag_chunk1 = sb("flag_chunk1", [P, 2, 6, HALF])
        KEEP, WEIGHT, START, SRC, SPARE, TARGET = range(6)
        table_row = sb("table_row", [P, HALF])
        spare_f = sb("spare_f", [P, 1])
        before_me = sb("before_me", [P, P])
        twins = sb("twins", [P, 2, BATCH])
        shift = sb("shift", [P, BATCH])
        pair_waste = sb("pair_waste", [P, 2, BATCH, P], BF16)
        target = sb("target", [P, SLOTS, BATCH], I32)
        window = sb("window", [P, P])
        window_t = sb("window_t", [P, P])
        first_chunk = sb("first_chunk", [P, GROUP], I32)
        first_edge = sb("first_edge", [P, NB], I32)
        spare_edge = sb("spare_edge", [P, NB])
        node_i = sb("node_i", [P, NB], I32)
        spread_ps = [bank[0], bank[3]]
        turned_ps = bank[0][:, 0:P]
        combined = [bank[1], bank[2]]

        def started(r, s):
            return bank[4 + 2 * r + s // 2][:, (s % 2) * D:(s % 2 + 1) * D]

        x0_loaded, x1_loaded, x_loaded, theta_loaded = (sem(f"{n}_loaded") for n in ("x0", "x1", "x", "theta"))
        edges_loaded, rows_loaded, mats_loaded = sem("edges_loaded"), sem("rows_loaded"), sem("mats_loaded")
        const_made, filled, iota_made = sem("const_made"), sem("filled"), sem("iota_made")
        pool_chain, dve_chain = sem("pool_chain"), sem("dve_chain")
        waited, dve_waited = sem("waited"), sem("dve_waited")
        wdiff_made, wt_turned, wt_ready = sem("wdiff_made"), sem("wt_turned"), sem("wt_ready")
        cols_ready = sem("cols_ready")
        p_stat, p_root, p_inverse, p_ln, p_norm = (sem(f"p_{n}") for n in ("stat", "root", "inverse", "ln", "norm"))
        p_turned, p_copied, p_product, p_evac = (sem(f"p_{n}") for n in ("turned", "copied", "product", "evac"))
        rows_stored = [sem(f"rows_stored{b}") for b in range(GROUP)]
        STORED = 16 * GROUPS
        gathered = [sem(f"gathered{r}") for r in range(SLOTS)]
        stored = [sem(f"stored{r}") for r in range(SLOTS)]
        idx_ready = sem("idx_ready")
        flag_ready = [sem(f"l{l}_flag_ready") for l in range(2)]
        folded = [sem(f"l{l}_folded") for l in range(2)]
        onehot_ready, onehot_used = sem("onehot_ready"), sem("onehot_used")
        s_norm, s_turned, s_copied, s_product, s_evac = (
            sem(f"side_{n}") for n in ("norm", "turned", "copied", "product", "evac"))
        side_done = sem("side_done")
        zeroed, zero_stored = sem("zeroed"), sem("zero_stored")
        start_gathered, start_ready, pairs_ready = sem("start_gathered"), sem("start_ready"), sem("pairs_ready")
        window_ready, window_turned, window_copied = sem("window_ready"), sem("window_turned"), sem("window_copied")
        src_spread, combined_ready, message_ready = sem("src_spread"), sem("combined_ready"), sem("message_ready")
        target_ready, table_free = sem("target_ready"), sem("table_free")
        sources_copied, shift_made = sem("sources_copied"), sem("shift_made")
        streamed = [sem(f"streamed{r}") for r in range(SLOTS)]
        scattered = [sem(f"scattered{r}") for r in range(TABLES)]
        hw_scattered = [sem(f"hw_scattered{b}") for b in range(GROUP)]
        own_made = sem("own_made")
        own_stored = [sem(f"own_stored{b}") for b in range(GROUP)]
        sums_loaded = [sem(f"sums_loaded{b}") for b in range(GROUP)]
        halved = sem("halved")
        zeros_made, hist_closed = sem("zeros_made"), sem("hist_closed")
        hist_copied, prefix_made, last_ready = sem("hist_copied"), sem("prefix_made"), sem("last_ready")
        gate_diag, gate_spread = sem("gate_diag"), sem("gate_spread")
        tail_turned = sem("tail_turned")
        carried = sem("carried")
        carry_turned = sem("carry_turned")
        fix_gathered = sem("fix_gathered")
        fix_made = sem("fix_made")
        fix_stored = sem("fix_stored")
        last_staged, first_staged = sem("last_staged"), sem("first_staged")
        n_gathered = [sem(f"n_gathered{b}") for b in range(GROUP)]
        n_comb, n_relu, n_x, n_stat, n_root, n_inverse, n_ln, n_norm, n_turned, n_copied, n_product, n_evac = (
            [sem(f"n{l}_{n}") for l in range(2)] for n in
            ("comb", "relu", "x", "stat", "root", "inverse", "ln", "norm", "turned", "copied", "product", "evac"))
        n_scaled, n_out = sem("n1_scaled"), sem("n1_out")

        block = ctx.enter_context(nc.Block())

        def over_blocks(eng, step, lag):
            for t in range(PEEL * GROUP):
                step(t, t % GROUP, t // GROUP)
            with eng.Fori(PEEL, GROUPS) as g:
                for b in range(GROUP):
                    step(g * GROUP + b, b, g)
            for t in range(NB, NB + lag):
                step(t, t % GROUP, t // GROUP)

        def uses(g, b, back):
            return g - 1 if b < back else g

        def live(t, back):
            return not isinstance(t, int) or 0 <= t - back < NB

        def later(t, n):
            return not isinstance(t, int) or t >= n

        def at(t, back):
            return t - back

        def blk(tile, t):
            if isinstance(t, int):
                return tile[:, t, :]
            return tile[:, bass.ds(t, 1), :].rearrange("p a d -> p (a d)")

        def col(tile, t, n=None):
            if n is None:
                return tile[:, t:t + 1] if isinstance(t, int) else tile[:, bass.ds(t, 1)]
            if isinstance(t, int):
                return tile[:, t, n:n + 1]
            return tile[:, bass.ds(t, 1), n:n + 1].rearrange("p a d -> p (a d)")

        @block.sync
        def _(sp):
            sp.wait_ge(filled, 1)
            x_blocks = x[0:NFULL * P, :].rearrange("(t p) d -> p t d", p=P)
            sp.dma_start(x_sb[:, 0:GROUP, :], x_blocks[:, 0:GROUP, :]).then_inc(x0_loaded, 16)
            sp.dma_start(w_nat[:, 0], theta_w.rearrange("(k p) d -> p k d", p=P)).then_inc(theta_loaded, 16)
            sp.dma_start(w_nat[:, 1], phi_w.rearrange("(k p) d -> p k d", p=P)).then_inc(theta_loaded, 16)
            for g in range(1, GROUPS):
                hi = min(g * GROUP + GROUP, NFULL)
                sp.dma_start(x_sb[:, g * GROUP:hi, :], x_blocks[:, g * GROUP:hi, :])\
                    .then_inc(x1_loaded if g == 1 else x_loaded, 16)
            sp.dma_start(x_sb[0:NREST, NFULL, :], x[NFULL * P:N, :]).then_inc(x_loaded, 16)

            def store_b(t, b, g):
                sp.wait_ge(p_evac, t + 1)
                sp.dma_start(table_b[bass.ds(t * P, P), :], rows_n[:, b, :]).then_inc(rows_stored[b], 16)
            over_blocks(sp, store_b, 0)

            tables = sums.rearrange("(r t p) d -> p r t d", r=TABLES, p=P)
            sp.wait_ge(zeroed, 1)
            sp.dma_start(tables[:, :, NB, :], zero_rows).then_inc(zero_stored, 16)
            with sp.Fori(0, ITERS) as i:
                for b in range(ITER_BATCHES):
                    r = b % SLOTS
                    k = (i * ITER_BATCHES + b) * BATCH
                    sp.wait_ge(folded[0], k + BATCH)
                    sp.dma_start(edge_rows[:, bass.ds(k, BATCH), :],
                                 sring[:, r * BATCH:(r + 1) * BATCH, :]).then_inc(stored[r], 16)
                    if b == 2:
                        sp.dma_start(tables[:, 1:TABLES, bass.ds(i, 1), :].rearrange("p r a d -> p (r a) d"),
                                     zero_rows[:, 1:TABLES]).then_inc(zero_stored, 16)
                    if b == 6:
                        sp.dma_start(states[bass.ds(i * P + P * CP, P), :], zero_rows[:, 0]).then_inc(zero_stored, 16)

            def store_hw(t, b, g):
                if live(t, 7):
                    u, c = at(t, 7), (b - 7) % GROUP
                    sp.wait_ge(n_evac[0], u + 1)
                    sp.dma_start(table_hw[bass.ds(u * P, P), :], rows_n[:, c, :]).then_inc(rows_stored[c], 16)
                    sp.wait_ge(own_made, u + 1)
                    sp.dma_start(sums[bass.ds(u * P, P), :], blk(a_sb, u)).then_inc(own_stored[c], 16)
            over_blocks(sp, store_hw, 7)

            for b in range(GROUP):
                sp.wait_ge(hw_scattered[b], 16 * GROUPS)

            def stream(i, first):
                for b in range(ITER_BATCHES):
                    r = b % SLOTS
                    n = i * ITER_BATCHES + b
                    if not first or b >= SLOTS:
                        sp.wait_ge(start_ready, n - SLOTS + 1)
                    sp.dma_start(gring[:, r * BATCH:(r + 1) * BATCH, :],
                                 edge_rows[:, bass.ds(n * BATCH, BATCH), :]).then_inc(streamed[r], 16)
            stream(0, True)
            with sp.Fori(1, ITERS) as i:
                stream(i, False)

            for r in range(TABLES):
                sp.wait_ge(scattered[r], 16 * CP // TABLES)

            def nodes1(t, b, g):
                if live(t, 0):
                    if later(t, GROUP):
                        sp.wait_ge(n_comb[1], t - GROUP + 1)
                    at_t = tables[:, :, t, :] if isinstance(t, int) else \
                        tables[:, :, bass.ds(t, 1), :].rearrange("p r a d -> p (r a) d")
                    sp.dma_start(block_sums[:, b], at_t).then_inc(sums_loaded[b], 16)
                if live(t, 8):
                    u, c = at(t, 8), (b - 8) % GROUP
                    rows = NREST if isinstance(u, int) and u == NFULL else P
                    sp.wait_ge(n_out, u + 1)
                    sp.dma_start(out[bass.ds(u * P, rows), :], rows_h[0:rows, c, :]).then_inc(rows_stored[c], 16)
            over_blocks(sp, nodes1, 8)
            for b in range(GROUP):
                sp.wait_ge(rows_stored[b], 3 * STORED)

        @block.gpsimd
        def _(pool):
            chained = [0]

            def chain(instruction):
                chained[0] += 1
                instruction.then_inc(pool_chain, 1)
                pool.wait_ge(pool_chain, chained[0])

            pool.memset(x_sb[:, NFULL, :], 0.0).then_inc(filled, 1)
            pool.memset(dst_i[:, :], PAD_DST).then_inc(filled, 1)
            pool.memset(src_sb[:, :], 0).then_inc(filled, 1)
            pool.memset(w_f, 0.0).then_inc(filled, 1)
            pool.memset(first_i[:, :], -1).then_inc(filled, 1)
            pool.memset(ones[:, :], 1.0).then_inc(const_made, 1)
            chain(pool.memset(ident[:, :], 0.0))
            pool.affine_select(out=ident[:, :], in_=ident[:, :], compare_op=ALU.not_equal, fill=1.0,
                               base=0, pattern=[[-1, P]], channel_multiplier=1).then_inc(const_made, 1)
            chain(pool.memset(upper[:, :], 1.0))
            pool.affine_select(out=upper[:, :], in_=upper[:, :], compare_op=ALU.is_ge, fill=0.0,
                               base=0, pattern=[[1, P]], channel_multiplier=-1).then_inc(const_made, 1)
            pool.iota(iota_i[:, :], pattern=[[1, P]], base=0, channel_multiplier=0).then_inc(iota_made, 1)
            pool.iota(row_i[:, :], pattern=[[0, 1]], base=0, channel_multiplier=CP).then_inc(iota_made, 1)
            pool.iota(node_i[:, :], pattern=[[P, NB]], base=P * CP, channel_multiplier=1).then_inc(iota_made, 1)
            chain(pool.memset(before_me[:, :], 1.0))
            pool.affine_select(out=before_me[:, :], in_=before_me[:, :], compare_op=ALU.is_gt, fill=0.0,
                               base=0, pattern=[[-1, P]], channel_multiplier=1).then_inc(const_made, 1)
            for s in range(HALF):
                last = pool.memset(table_row[:, s:s + 1], float(s % TABLES * ROWS))
            last.then_inc(const_made, 1)
            pool.wait_ge(x_loaded, 16 * (GROUPS - 1))
            pool.wait_ge(filled, 5)
            for tile, array in ((dst_i, dst), (src_sb, src), (w_f, edge_weight)):
                pool.dma_start(tile[0:PFULL, 0:CP], array[0:PFULL * CP].rearrange("(p k) -> p k", k=CP))\
                    .then_inc(edges_loaded, 16)
                pool.dma_start(tile[PFULL:P, 0:PREST], array[PFULL * CP:E].rearrange("(p k) -> p k", p=1))\
                    .then_inc(edges_loaded, 16)
            with nc.allow_non_contiguous_dma(reason="one element per partition"):
                pool.dma_start(first_i[1:P, :], dst[0:(P - 1) * CP].rearrange("(p k) -> p k", k=CP)[:, CP - 1:CP])\
                    .then_inc(edges_loaded, 16)
            for tile, array in ((b1_rows, b1), (off_rows, offset), (scale_rows, scale), (eps1, eps)):
                pool.dma_start(tile[:, :], array.partition_broadcast(P)).then_inc(rows_loaded, 16)
            for tile, array in ((bias_a[:, 0, :], theta_b), (bias_a[:, 1, :], phi_b), (b2_row[:, :], b2)):
                pool.dma_start(tile, array.rearrange("(a d) -> a d", a=1)).then_inc(rows_loaded, 16)
            pool.dma_start(w1_sb[:, :, :], w1.rearrange("(k p) d -> p k d", p=P)).then_inc(mats_loaded, 16)
            pool.dma_start(w2_sb[:, :, :], w2.rearrange("(k p) d -> p k d", p=P)).then_inc(mats_loaded, 16)

            def gather_edges(i, first):
                for b in range(ITER_BATCHES):
                    r, h = b % SLOTS, b * BATCH // HALF
                    if not first or b >= SLOTS:
                        pool.wait_ge(folded[0], (i * ITER_BATCHES + b - SLOTS + 1) * BATCH)
                    if b * BATCH % HALF == 0:
                        pool.wait_ge(idx_ready, 2 * i + h + 1)
                    pool.sem_inc(waited, 1)
                    for s in range(BATCH):
                        k = (b * BATCH + s) % HALF
                        pool.indirect_dma_start(
                            gring[:, r * BATCH + s, :], None, table_b,
                            bass.IndirectOffsetOnAxis(ap=idx_chunk[:, h, k:k + 1], axis=0)).then_inc(gathered[r], 16)
            for b in range(GROUP):
                pool.wait_ge(rows_stored[b], STORED)
            gather_edges(0, True)
            with pool.Fori(1, ITERS) as i:
                gather_edges(i, False)

            pool.wait_ge(cols_ready, 1)
            for r in range(SLOTS):
                pool.wait_ge(stored[r], 16 * CP // BATCH // SLOTS)
            pool.indirect_dma_start(rows_h[:, 0, :], None, states,
                                    bass.IndirectOffsetOnAxis(ap=fix_i[:, 0:1], axis=0)).then_inc(fix_gathered, 16)
            pool.wait_ge(fix_made, 1)
            pool.indirect_dma_start(states, bass.IndirectOffsetOnAxis(ap=fix_i[:, 0:1], axis=0),
                                    rows_h[:, 1, :], None).then_inc(fix_stored, 16)
            pool.wait_ge(fix_stored, 16)
            pool.wait_ge(zero_stored, 16 * (2 * ITERS + 1))
            pool.wait_ge(last_ready, 1)

            def nodes0(t, b, g):
                if live(t, 0):
                    if later(t, GROUP):
                        pool.wait_ge(n_comb[0], t - GROUP + 1)
                        pool.wait_ge(last_staged, t - GROUP + 1)
                if live(t, 7):
                    u, c = at(t, 7), (b - 7) % GROUP
                    pool.wait_ge(first_staged, u + 1)
                    pool.wait_ge(n_evac[0], u + 1)
                pool.sem_inc(waited, 1)
                if live(t, 0):
                    pool.indirect_dma_start(rows_in[:, b, :], None, states,
                                            bass.IndirectOffsetOnAxis(ap=last_chunk[:, b:b + 1], axis=0))\
                        .then_inc(n_gathered[b], 16)
                if live(t, 7):
                    pool.indirect_dma_start(states, bass.IndirectOffsetOnAxis(ap=first_chunk[:, c:c + 1], axis=0),
                                            rows_n[:, c, :], None).then_inc(hw_scattered[c], 16)
            over_blocks(pool, nodes0, 7)

            for b in range(GROUP):
                pool.wait_ge(rows_stored[b], 2 * STORED)
            pool.indirect_dma_start(sring[:, SLOTS * BATCH - 1, :], None, table_hw,
                                    bass.IndirectOffsetOnAxis(ap=start_dst[:, :], axis=0)).then_inc(start_gathered, 16)
            for b in range(GROUP):
                pool.wait_ge(own_stored[b], 16 * GROUPS)

            def scatter_edges(i, first):
                for b in range(ITER_BATCHES):
                    n = i * ITER_BATCHES + b
                    pool.wait_ge(message_ready, 2 * n + 2)
                    pool.wait_ge(target_ready, n + 1)
                    for s in range(BATCH):
                        if not first or b > 0:
                            pool.wait_ge(scattered[s], 16 * n)
                        pool.sem_inc(table_free, 1)
                        pool.indirect_dma_start(
                            sums, bass.IndirectOffsetOnAxis(ap=target[:, b % SLOTS, s:s + 1], axis=0),
                            message[:, b % SLOTS * BATCH + s, :], None, compute_op=ALU.add).then_inc(scattered[s], 16)
            scatter_edges(0, True)
            with pool.Fori(1, ITERS) as i:
                scatter_edges(i, False)

            def nodes1(t, b, g):
                if live(t, 2):
                    u, c = at(t, 2), (b - 2) % GROUP
                    pool.wait_ge(sums_loaded[c], 16 * (uses(g, b, 2) + 1))
                    pool.tensor_tensor(block_sums[:, c, 0:2], block_sums[:, c, 0:2], block_sums[:, c, 2:4], ALU.add)\
                        .then_inc(halved, 1)
            over_blocks(pool, nodes1, 2)

        @block.scalar
        def _(act):
            def root(stat, done, t, b, layer):
                act.wait_ge(stat, 2 * t + 2)
                act.activation(std[:, b:b + 1], mv[:, b, 1:2], ACT.Sqrt, bias=ln_eps[:, layer:layer + 1])\
                    .then_inc(done, 1)

            def prelude(t, b, g):
                if live(t, 2):
                    u, c = at(t, 2), (b - 2) % GROUP
                    act.wait_ge(p_ln, u + 1)
                    if later(u, GROUP):
                        act.wait_ge(p_turned, u - GROUP + 1)
                    act.activation(rows_u[:, c, :], blk(x_sb, u), ACT.Relu, bias=col(ln, u, 1), scale=col(ln, u, 0))\
                        .then_inc(p_norm, 1)
                if live(t, 4):
                    u, c = at(t, 4), (b - 4) % GROUP
                    act.wait_ge(p_product, u + 1)
                    if later(u, GROUP):
                        act.wait_ge(rows_stored[c], 16 * uses(g, b, 4))
                    act.activation(rows_n[:, c, :], mm[c % 2], ACT.Copy).then_inc(p_evac, 1)
                if live(t, 0):
                    root(p_stat, p_root, t, b, 0)
            act.wait_ge(zeros_made, 3)
            act.wait_ge(wt_ready, 2)
            over_blocks(act, prelude, 4)

            def iteration0(i, first):
                for h in range(2):
                    u = 2 * i + h
                    if not (first and h == 0):
                        act.wait_ge(folded[0], u * HALF)
                    act.activation(idx_chunk[:, 1 - h, :], src_sb[:, bass.ds((u + 1) * HALF, HALF)], ACT.Copy)\
                        .then_inc(idx_ready, 1)
                    if not first:
                        act.wait_ge(onehot_ready, (u - 1) * (HALF // BATCH))
                    if first and h == 0:
                        act.wait_ge(cols_ready, 1)
                    f = flags[:, u, 0:3, :] if isinstance(u, int) else \
                        flags[:, bass.ds(u, 1), 0:3, :].rearrange("p a k s -> p (a k) s")
                    act.activation(flag_chunk[:, h], f, ACT.Copy).then_inc(flag_ready[0], 1)
                    if h == 0:
                        if not first:
                            act.wait_ge(s_turned, i)
                        act.activation(hst[:, 0, :], blk(x_sb, i), ACT.Relu, bias=col(ln, i, 1), scale=col(ln, i, 0))\
                            .then_inc(s_norm, 1)
                        act.wait_ge(s_turned, i + 1)
                        if not first:
                            act.wait_ge(s_product, i)
                        act.activation(hst[:, 1, :], tp[0], ACT.Copy).then_inc(s_copied, 1)
                    else:
                        act.wait_ge(s_product, i + 1)
                        act.activation(blk(a_sb, i), mm[0], ACT.Copy).then_inc(s_evac, 1)

            act.wait_ge(edges_loaded, 16 * 7)
            act.activation(idx_chunk[:, 0, :], src_sb[:, 0:HALF], ACT.Copy).then_inc(idx_ready, 1)
            iteration0(0, True)
            with act.Fori(1, ITERS) as i:
                iteration0(i, False)

            def nodes0(t, b, g):
                if live(t, 4):
                    root(n_stat[0], n_root[0], at(t, 4), (b - 4) % GROUP, 0)
                if live(t, 2):
                    u, c = at(t, 2), (b - 2) % GROUP
                    act.wait_ge(n_comb[0], u + 1)
                    act.activation(rows_u[:, c, :], rows_u[:, c, :], ACT.Relu, scale=col(has, u)).then_inc(n_relu[0], 1)
                if live(t, 5):
                    u, c = at(t, 5), (b - 5) % GROUP
                    act.wait_ge(n_turned[0], u + 1)
                    if later(u, GROUP):
                        act.wait_ge(n_product[0], u - GROUP + 1)
                    act.activation(rows_t[:, c, :], tp[c % 2], ACT.Copy).then_inc(n_copied[0], 1)
                if live(t, 4):
                    u, c = at(t, 4), (b - 4) % GROUP
                    act.wait_ge(n_ln[0], u + 1)
                    if later(u, GROUP):
                        act.wait_ge(n_turned[0], u - GROUP + 1)
                    act.activation(rows_h[:, c, :], blk(x_sb, u), ACT.Relu, bias=col(ln, u, 1), scale=col(ln, u, 0))\
                        .then_inc(n_norm[0], 1)
                if live(t, 6):
                    u, c = at(t, 6), (b - 6) % GROUP
                    act.wait_ge(n_product[0], u + 1)
                    if later(u, GROUP):
                        act.wait_ge(rows_stored[c], STORED + 16 * uses(g, b, 6))
                        act.wait_ge(hw_scattered[c], 16 * uses(g, b, 6))
                        act.wait_ge(own_made, u - GROUP + 1)
                    act.activation(rows_n[:, c, :], mm[c % 2], ACT.Copy).then_inc(n_evac[0], 1)
            act.wait_ge(fix_stored, 16)
            act.wait_ge(zero_stored, 16 * (2 * ITERS + 1))
            over_blocks(act, nodes0, 6)

            def stage1(u, h, first):
                if not first:
                    act.wait_ge(target_ready, (u - 1) * (HALF // BATCH))
                f = flags[:, u, 3:5, :] if isinstance(u, int) else \
                    flags[:, bass.ds(u, 1), 3:5, :].rearrange("p a k s -> p (a k) s")
                k = flags[:, u, 3, :] if isinstance(u, int) else \
                    flags[:, bass.ds(u, 1), 3, :].rearrange("p a s -> p (a s)")
                now = src_sb[:, bass.ds(u * HALF, HALF)]
                act.activation(flag_chunk1[:, h, 0:2], f, ACT.Copy)
                act.activation(flag_chunk1[:, h, START], k, ACT.Copy, bias=1.0, scale=-1.0)
                act.activation(flag_chunk1[:, h, SRC], now, ACT.Copy)
                act.activation(flag_chunk1[:, h, SPARE], now, ACT.Identity, bias=spare_f[:, 0:1], scale=-1.0)\
                    .then_inc(flag_ready[1], 1)

            def messages(n, b, first):
                for j in range(2):
                    act.wait_ge(combined_ready, 2 * n + j + 1)
                    if j == 0 and not first:
                        act.wait_ge(table_free, (n - 2) * BATCH)
                    k = b % SLOTS * BATCH + 2 * j
                    act.activation(message[:, k:k + 2, :].rearrange("p s d -> p (s d)"), combined[j][:, :], ACT.Copy)\
                        .then_inc(message_ready, 1)

            def window_in(i):
                act.activation(window[:, :], src_sb[:, bass.ds(i * ITER_STEPS, P)], ACT.Copy).then_inc(window_ready, 1)

            def window_out(i):
                act.wait_ge(window_turned, i + 1)
                act.activation(window_t[:, :], turned_ps, ACT.Copy).then_inc(window_copied, 1)

            def iteration1(i, first):
                for b in range(ITER_BATCHES):
                    n, h = i * ITER_BATCHES + b, b * BATCH // HALF
                    if b * BATCH % HALF == 0:
                        stage1(2 * i + h, h, first)
                        act.wait_ge(flag_ready[1], 2 * i + h + 1)
                    act.wait_ge(streamed[b % SLOTS], 16 * (2 * i + b // SLOTS + 1))
                    if not first or b >= 2:
                        act.wait_ge(folded[1], (n - 1) * BATCH)
                    for s in range(BATCH):
                        k = (b * BATCH + s) % HALF
                        last = act.activation(started(b % 2, s), gring[:, b % SLOTS * BATCH + s, :], ACT.Copy,
                                              scale=flag_chunk1[:, h, START, k:k + 1])
                    last.then_inc(start_ready, 1)
                    if b == 0:
                        window_out(i)
                    if not first or b >= 2:
                        messages(n - 2, (b - 2) % SLOTS, first and b < 2 + SLOTS)
                    act.wait_ge(src_spread, n + 1)
                    if not first or b >= 2:
                        act.wait_ge(pairs_ready, n - 1)
                    act.activation(sources[:, b % 2].rearrange("p s q -> p (s q)"), spread_ps[b % 2][:, :], ACT.Copy)\
                        .then_inc(sources_copied, 1)
                    if b == SLOTS:
                        window_in(i + 1)
            act.wait_ge(own_made, NB)
            for b in range(GROUP):
                act.wait_ge(own_stored[b], 16 * GROUPS)
            window_in(0)
            iteration1(0, True)
            with act.Fori(1, ITERS) as i:
                iteration1(i, False)
            window_out(ITERS)
            messages(CP // BATCH - 2, SLOTS - 2, False)
            messages(CP // BATCH - 1, SLOTS - 1, False)

            def nodes1(t, b, g):
                if live(t, 4):
                    u, c = at(t, 4), (b - 4) % GROUP
                    act.wait_ge(n_turned[1], u + 1)
                    if later(u, GROUP):
                        act.wait_ge(n_product[1], u - GROUP + 1)
                    act.activation(rows_t[:, c, :], tp[c % 2], ACT.Relu).then_inc(n_copied[1], 1)
                if live(t, 5):
                    u, c = at(t, 5), (b - 5) % GROUP
                    act.wait_ge(n_product[1], u + 1)
                    if later(u, GROUP):
                        act.wait_ge(n_scaled, u - GROUP + 1)
                    act.activation(rows_n[:, c, :], mm[c % 2], ACT.Relu).then_inc(n_evac[1], 1)
                if live(t, 6):
                    u, c = at(t, 6), (b - 6) % GROUP
                    act.wait_ge(n_ln[1], u + 1)
                    act.activation(rows_n[:, c, :], rows_n[:, c, :], ACT.Identity, bias=col(ln, u, 1),
                                   scale=col(ln, u, 0)).then_inc(n_norm[1], 1)
                if live(t, 5):
                    root(n_stat[1], n_root[1], at(t, 5), (b - 5) % GROUP, 1)
            over_blocks(act, nodes1, 6)

        @block.tensor
        def _(pe):
            pe.wait_ge(const_made, 5)
            for m in range(2):
                pe.wait_ge(wdiff_made if m == 0 else theta_loaded, 1 if m == 0 else 32)
                if m == 1:
                    pe.wait_ge(wt_ready, 1)
                for k in range(KH):
                    for n in range(KH):
                        last = pe.transpose(tp[k][:, n * P:(n + 1) * P],
                                            w_nat[:, 1 - m, n, k * P:(k + 1) * P], ident[:, :])
                last.then_inc(wt_turned, 1)

            def turn(bank_ap, rows, done):
                for k in range(KH):
                    last = pe.transpose(bank_ap[:, k * P:(k + 1) * P], rows[:, k * P:(k + 1) * P], ident[:, :])
                last.then_inc(done, 1)

            def product(bank_ap, rows_turned, weights, done, bias=()):
                for k in range(KH):
                    last = pe.matmul(bank_ap, rows_turned[:, k * P:(k + 1) * P], weights[:, k, :],
                                     start=(k == 0), stop=(k == KH - 1 and not bias))
                for n, row in enumerate(bias):
                    last = pe.matmul(bank_ap, ones[0:1, :], row, start=False, stop=(n == len(bias) - 1))
                last.then_inc(done, 1)

            pe.wait_ge(wt_ready, 2)

            def prelude(t, b, g):
                if live(t, 3):
                    u, c = at(t, 3), (b - 3) % GROUP
                    pe.wait_ge(p_norm, u + 1)
                    if later(u, 1 if c == 0 else 2):
                        pe.wait_ge(p_copied, u if c == 0 else u - 1)
                    turn(tp[c % 2], rows_u[:, c, :], p_turned)
                if live(t, 4):
                    u, c = at(t, 4), (b - 4) % GROUP
                    pe.wait_ge(p_copied, u + 1)
                    if later(u, 1 if c == 0 else 2):
                        pe.wait_ge(p_evac, u if c == 0 else u - 1)
                    product(mm[c % 2], rows_t[:, c, :], wb_t, p_product)
            over_blocks(pe, prelude, 4)

            def iteration0(i, first):
                pe.wait_ge(s_norm, i + 1)
                if not first:
                    pe.wait_ge(s_copied, i)
                else:
                    pe.wait_ge(p_copied, NB)
                turn(tp[0], hst[:, 0, :], s_turned)
                for b in range(ITER_BATCHES):
                    pe.wait_ge(onehot_ready, i * ITER_BATCHES + b + 1)
                    for s in range(BATCH):
                        last = pe.matmul(hist_ps, onehot[:, b % 2, s, 0:P], onehot[:, b % 2, s, P:P + NB],
                                         start=(first and b == 0 and s == 0), stop=False)
                    last.then_inc(onehot_used, 1)
                    if b == 2:
                        pe.wait_ge(s_copied, i + 1)
                        if not first:
                            pe.wait_ge(s_evac, i)
                        else:
                            pe.wait_ge(p_evac, NB)
                        product(mm[0], hst[:, 1, :], wa_t, s_product, (bias_a[:, 0, :], bias_a[:, 1, :]))
            pe.wait_ge(rows_loaded, 16 * 7)
            iteration0(0, True)
            with pe.Fori(1, ITERS) as i:
                iteration0(i, False)
            pe.wait_ge(zeros_made, 1)
            pe.matmul(hist_ps, zeros[:, :], zeros[:, 0:NB], start=False, stop=True).then_inc(hist_closed, 1)

            pe.wait_ge(hist_copied, 1)
            pe.matmul(bank[4][:, 0:NB], upper[:, :], hist[:, :], start=True, stop=True)
            pe.matmul(bank[4][:, 64:64 + NB], ones[:, :], hist[:, :], start=True, stop=True).then_inc(prefix_made, 1)
            pe.wait_ge(gate_diag, 1)
            pe.matmul(bank[5][:, 0:P], ones[:, :], hst[:, 0, 0:P], start=True, stop=True).then_inc(gate_spread, 1)

            pe.wait_ge(s_evac, ITERS)
            pe.wait_ge(folded[0], CP)
            turn(tp[0], sring[:, SLOTS * BATCH - 1, :], tail_turned)
            pe.wait_ge(carried, 1)
            for k in range(KH):
                last = pe.transpose(mm[0][:, k * P:(k + 1) * P], carry_t[:, k, 0:P], ident[:, :])
            last.then_inc(carry_turned, 1)
            pe.wait_ge(fix_made, 1)

            def nodes0(t, b, g):
                if live(t, 5):
                    u, c = at(t, 5), (b - 5) % GROUP
                    pe.wait_ge(n_norm[0], u + 1)
                    if later(u, 1 if c == 0 else 2):
                        pe.wait_ge(n_copied[0], u if c == 0 else u - 1)
                    turn(tp[c % 2], rows_h[:, c, :], n_turned[0])
                if live(t, 6):
                    u, c = at(t, 6), (b - 6) % GROUP
                    pe.wait_ge(n_copied[0], u + 1)
                    if later(u, 1 if c == 0 else 2):
                        pe.wait_ge(n_evac[0], u if c == 0 else u - 1)
                    product(mm[c % 2], rows_t[:, c, :], w1_sb, n_product[0])
            pe.wait_ge(mats_loaded, 32)
            over_blocks(pe, nodes0, 6)

            def turn_window(i):
                pe.wait_ge(window_ready, i + 1)
                pe.transpose(turned_ps, window[:, :], ident[:, :]).then_inc(window_turned, 1)
                pe.wait_ge(window_copied, i + 1)

            def spread(n, b):
                for s in range(BATCH):
                    k = b * BATCH + s
                    last = pe.matmul(spread_ps[b % 2][:, s * P:(s + 1) * P], ident[:, k:k + 1].to_broadcast([P, P]),
                                     window_t[:, :], start=True, stop=True)
                last.then_inc(src_spread, 1)

            def iteration1(i, first):
                for b in range(ITER_BATCHES):
                    n = i * ITER_BATCHES + b
                    if not (first and b == 0):
                        pe.wait_ge(sources_copied, n)
                    if b == ITER_BATCHES - 1:
                        turn_window(i + 1)
                    spread(n + 1, (b + 1) % ITER_BATCHES)
                    pe.wait_ge(pairs_ready, n + 1)
                    pe.wait_ge(folded[1], (n + 1) * BATCH)
                    for j in range(2):
                        if not (first and b == 0):
                            pe.wait_ge(message_ready, 2 * n + j - 1)
                        for s in (2 * j, 2 * j + 1):
                            last = pe.matmul(combined[j][:, s % 2 * D:(s % 2 + 1) * D], pairs[:, b % 2, s, :],
                                             sring[:, b % SLOTS * BATCH + s, :], start=True, stop=True)
                        last.then_inc(combined_ready, 1)
            pe.wait_ge(n_evac[0], NB)
            turn_window(0)
            spread(0, 0)
            iteration1(0, True)
            with pe.Fori(1, ITERS) as i:
                iteration1(i, False)
            pe.wait_ge(message_ready, 2 * CP // BATCH)

            def nodes1(t, b, g):
                if live(t, 3):
                    u, c = at(t, 3), (b - 3) % GROUP
                    pe.wait_ge(n_comb[1], u + 1)
                    if later(u, 1 if c == 0 else 2):
                        pe.wait_ge(n_copied[1], u if c == 0 else u - 1)
                    turn(tp[c % 2], rows_u[:, c, :], n_turned[1])
                if live(t, 4):
                    u, c = at(t, 4), (b - 4) % GROUP
                    pe.wait_ge(n_copied[1], u + 1)
                    if later(u, 1 if c == 0 else 2):
                        pe.wait_ge(n_evac[1], u if c == 0 else u - 1)
                    product(mm[c % 2], rows_t[:, c, :], w2_sb, n_product[1], (b2_row[:, :],))
            over_blocks(pe, nodes1, 4)

        @block.vector
        def _(dve):
            chained = [0]

            def chain(instruction):
                chained[0] += 1
                instruction.then_inc(dve_chain, 1)
                dve.wait_ge(dve_chain, chained[0])

            dve.memset(zeros[:, :], 0.0).then_inc(zeros_made, 1)
            dve.memset(ln_eps[:, 0:1], LN_EPS).then_inc(zeros_made, 1)
            dve.memset(ln_eps[:, 1:2], OUT_EPS).then_inc(zeros_made, 1)
            dve.wait_ge(theta_loaded, 32)
            dve.tensor_tensor(w_nat[:, 1], w_nat[:, 1], w_nat[:, 0], ALU.subtract).then_inc(wdiff_made, 1)
            for m, tile in enumerate((wb_t, wa_t)):
                dve.wait_ge(wt_turned, m + 1)
                for k in range(KH):
                    last = dve.tensor_copy(tile[:, k, :], tp[k])
                last.then_inc(wt_ready, 1)

            def sums_of(rows, stat, t, b):
                dve.sem_inc(dve_waited, 1)
                dve.bn_stats(bn[:, b, :], rows).then_inc(stat, 1)

            def moments(stat, t, b):
                dve.wait_ge(stat, 2 * t + 1)
                dve.sem_inc(dve_waited, 1)
                dve.bn_aggr(mv[:, b, :], bn[:, b, :]).then_inc(stat, 1)

            def inverse_of(root, inverse, t, b):
                dve.wait_ge(root, t + 1)
                dve.reciprocal(col(ln, t, 0), std[:, b:b + 1]).then_inc(inverse, 1)

            def shift_by_mean(inverse, done, t, b):
                dve.wait_ge(inverse, t + 1)
                dve.scalar_tensor_tensor(col(ln, t, 1), mv[:, b, 0:1], -1.0, col(ln, t, 0), ALU.mult, ALU.mult)\
                    .then_inc(done, 1)

            def prelude(t, b, g):
                if live(t, 2):
                    inverse_of(p_root, p_inverse, at(t, 2), (b - 2) % GROUP)
                if live(t, 0):
                    if isinstance(t, int):
                        if t in (0, GROUP):
                            dve.wait_ge(x1_loaded if t else x0_loaded, 16)
                    elif b == 0:
                        dve.wait_ge(x_loaded, 16 * (GROUPS - 1))
                    sums_of(blk(x_sb, t), p_stat, t, b)
                if live(t, 2):
                    shift_by_mean(p_inverse, p_ln, at(t, 2), (b - 2) % GROUP)
                if live(t, 0):
                    moments(p_stat, t, b)
                if live(t, 3):
                    u, c = at(t, 3), (b - 3) % GROUP
                    dve.wait_ge(p_turned, u + 1)
                    if later(u, GROUP):
                        dve.wait_ge(p_product, u - GROUP + 1)
                    dve.tensor_copy(rows_t[:, c, :], tp[c % 2]).then_inc(p_copied, 1)
            over_blocks(dve, prelude, 3)

            dve.wait_ge(edges_loaded, 16 * 7)
            dve.wait_ge(iota_made, 3)
            chain(dve.tensor_copy(iota_f[:, :], iota_i[:, :]))
            chain(dve.tensor_copy(row_f[:, :], row_i[:, :]))
            dve.tensor_copy(dst_f[:, 0:1], first_i[:, :])
            dve.tensor_copy(start_dst[:, :], dst_i[:, 0:1])
            chain(dve.tensor_copy(dst_f[:, 1:CP + 1], dst_i[:, :]))
            now = dst_f[:, 1:CP + 1].rearrange("p (h s) -> p h s", s=HALF)
            before = dst_f[:, 0:CP].rearrange("p (h s) -> p h s", s=HALF)
            chain(dve.tensor_tensor(flags[:, :, 3, :], now, before, ALU.is_equal))
            chain(dve.tensor_copy(cont, flags[:, 0, 3, 0:1]))
            chain(dve.memset(flags[:, 0, 3, 0:1], 0.0))
            chain(dve.tensor_scalar(flags[:, :, 0, :], flags[:, :, 3, :], -1.0, BIG, ALU.add, ALU.mult))
            dve.memset(flags[:, 0, 3, 0:1], 1.0)
            dve.tensor_copy(spare_edge[:, :], node_i[:, :])
            chain(dve.tensor_copy(spare_f[:, :], node_i[:, 0:1]))
            chain(dve.tensor_scalar(spare_f[:, :], spare_f[:, :], float(NB * P - P * CP), None, ALU.add))
            dve.tensor_copy(flags[:, :, 4, :], w_f.rearrange("p (h s) -> p h s", s=HALF))
            halves = dst_s.rearrange("p (h s) -> p h s", s=HALF)
            chain(dve.tensor_scalar(dst_s, dst_i[:, :], 7, None, ALU.arith_shift_right))
            chain(dve.tensor_copy(flags[:, :, 1, :], halves))
            chain(dve.tensor_scalar(dst_s, dst_i[:, :], P - 1, None, ALU.bitwise_and))
            chain(dve.tensor_copy(flags[:, :, 2, :], halves))
            same = dst_s.bitcast(F32)
            chain(dve.tensor_scalar(same, dst_f[:, 1:CP + 1], dst_f[:, 1:2], None, ALU.is_equal))
            chain(dve.tensor_reduce(nfirst, same, AX.X, ALU.add))
            chain(dve.tensor_copy(whole, same[:, CP - 1:CP]))
            chain(dve.tensor_tensor(gate, cont, whole, ALU.mult))
            dve.tensor_scalar(cont_neg, cont, -1.0, BIG, ALU.add, ALU.mult)
            chain(dve.scalar_tensor_tensor(fix_f, nfirst, -1.0, row_f[:, :], ALU.add, ALU.add))
            dve.tensor_copy(fix_i[:, :], fix_f).then_inc(cols_ready, 1)

            def iteration0(i, first):
                for b in range(ITER_BATCHES):
                    r, h = b % SLOTS, b * BATCH // HALF
                    n = i * ITER_BATCHES + b
                    if b * BATCH % HALF == 0:
                        dve.wait_ge(flag_ready[0], 2 * i + h + 1)
                    if not first or b >= 2:
                        dve.wait_ge(onehot_used, n - 1)
                    if not first or b >= SLOTS:
                        dve.wait_ge(stored[r], 16 * (2 * i + b // SLOTS))
                    dve.wait_ge(gathered[r], 16 * BATCH * (2 * i + b // SLOTS + 1))
                    for s in range(BATCH):
                        k = (b * BATCH + s) % HALF
                        if not (first and b == 0 and s == 0):
                            dve.wait_ge(folded[0], n * BATCH + s)
                        dve.scalar_tensor_tensor(sring[:, r * BATCH + s, :],
                                                 sring[:, (r * BATCH + s - 1) % (SLOTS * BATCH), :],
                                                 flag_chunk[:, h, 0, k:k + 1], gring[:, r * BATCH + s, :],
                                                 ALU.add, ALU.max).then_inc(folded[0], 1)
                        dve.tensor_scalar(onehot[:, b % 2, s, 0:P], iota_f[:, :], flag_chunk[:, h, 2, k:k + 1],
                                          None, ALU.is_equal)
                        last = dve.tensor_scalar(onehot[:, b % 2, s, P:P + NB], iota_f[:, 0:NB],
                                                 flag_chunk[:, h, 1, k:k + 1], None, ALU.is_equal)
                    last.then_inc(onehot_ready, 1)
            for b in range(GROUP):
                dve.wait_ge(rows_stored[b], STORED)
            dve.memset(zero_rows, 0.0).then_inc(zeroed, 1)
            chain(dve.memset(sring[:, SLOTS * BATCH - 1, :], 0.0))
            iteration0(0, True)
            with dve.Fori(1, ITERS) as i:
                iteration0(i, False)

            dve.wait_ge(hist_closed, 1)
            chain(dve.tensor_copy(hist[:, :], hist_ps))
            dve.tensor_scalar(has[:, :], hist[:, :], 0.0, None, ALU.is_gt).then_inc(hist_copied, 1)
            chain(dve.memset(cum[:, 0:1], -1.0))
            dve.wait_ge(hist_copied, 1)
            dve.wait_ge(prefix_made, 1)
            one_row = ones[:, 0:NB]
            chain(dve.tensor_tensor_scan(cum[:, 1:NB + 1], one_row, bank[4][:, 64:64 + NB], -1.0, ALU.mult, ALU.add))
            chain(dve.tensor_tensor(last_f[:, :], bank[4][:, 0:NB], cum[:, 0:NB], ALU.add))
            chain(dve.tensor_tensor(last_f[:, :], last_f[:, :], spare_edge[:, :], ALU.subtract))
            chain(dve.scalar_tensor_tensor(hist[:, :], hist[:, :], -1.0, last_f[:, :], ALU.mult, ALU.add))
            chain(dve.tensor_tensor(last_f[:, :], last_f[:, :], has[:, :], ALU.mult))
            chain(dve.scalar_tensor_tensor(hist[:, :], hist[:, :], 1.0, has[:, :], ALU.add, ALU.mult))
            dve.memset(last_i[:, NB:NB + GROUP], 0)
            chain(dve.tensor_tensor(first_edge[:, :], hist[:, :], spare_edge[:, :], ALU.add))
            chain(dve.tensor_tensor(last_i[:, 0:NB], last_f[:, :], spare_edge[:, :], ALU.add))
            dve.tensor_copy(last_chunk[:, :], last_i[:, 0:GROUP]).then_inc(last_ready, 1)
            dve.wait_ge(s_copied, ITERS)
            dve.tensor_scalar(hst[:, 0, 0:P], ident[:, :], gate, None, ALU.mult).then_inc(gate_diag, 1)
            dve.wait_ge(gate_spread, 1)
            chain(dve.tensor_scalar(gate_rows[:, :], bank[5][:, 0:P], -1.0, BIG, ALU.add, ALU.mult))

            dve.memset(carry_t[:, :, 0:1], 0.0)
            dve.wait_ge(tail_turned, 1)
            for k in range(KH):
                last = dve.tensor_tensor_scan(carry_t[:, k, 1:P + 1], gate_rows[:, :],
                                              tp[0][:, k * P:(k + 1) * P], 0.0, ALU.add, ALU.max)
            last.then_inc(carried, 1)
            dve.wait_ge(carry_turned, 1)
            dve.wait_ge(fix_gathered, 16)
            dve.scalar_tensor_tensor(rows_h[:, 1, :], mm[0], cont_neg, rows_h[:, 0, :], ALU.add, ALU.max)\
                .then_inc(fix_made, 1)

            def nodes0(t, b, g):
                if live(t, 3):
                    u, c = at(t, 3), (b - 3) % GROUP
                    dve.wait_ge(n_relu[0], u + 1)
                    dve.tensor_tensor(blk(x_sb, u), blk(x_sb, u), rows_u[:, c, :], ALU.add).then_inc(n_x[0], 1)
                if live(t, 2):
                    u, c = at(t, 2), (b - 2) % GROUP
                    dve.wait_ge(n_gathered[c], 16 * (uses(g, b, 2) + 1))
                    if later(u, GROUP):
                        dve.wait_ge(n_x[0], u - GROUP + 1)
                    dve.tensor_tensor(rows_u[:, c, :], rows_in[:, c, :], blk(a_sb, u), ALU.add).then_inc(n_comb[0], 1)
                    dve.tensor_copy(last_chunk[:, c:c + 1], col(last_i, u + GROUP)).then_inc(last_staged, 1)
                if live(t, 4):
                    inverse_of(n_root[0], n_inverse[0], at(t, 4), (b - 4) % GROUP)
                if live(t, 3):
                    u, c = at(t, 3), (b - 3) % GROUP
                    dve.wait_ge(n_x[0], u + 1)
                    sums_of(blk(x_sb, u), n_stat[0], u, c)
                if live(t, 4):
                    u, c = at(t, 4), (b - 4) % GROUP
                    if later(u, GROUP):
                        dve.wait_ge(hw_scattered[c], 16 * uses(g, b, 4))
                    dve.tensor_copy(first_chunk[:, c:c + 1], col(first_edge, u)).then_inc(first_staged, 1)
                if live(t, 4):
                    shift_by_mean(n_inverse[0], n_ln[0], at(t, 4), (b - 4) % GROUP)
                if live(t, 7):
                    u, c = at(t, 7), (b - 7) % GROUP
                    dve.wait_ge(n_evac[0], u + 1)
                    dve.scalar_tensor_tensor(blk(a_sb, u), rows_n[:, c, :], eps1[:, 0:1], b1_rows[:, :],
                                             ALU.mult, ALU.add).then_inc(own_made, 1)
                if live(t, 3):
                    moments(n_stat[0], at(t, 3), (b - 3) % GROUP)
            dve.wait_ge(s_evac, ITERS)
            dve.wait_ge(rows_loaded, 16 * 7)
            chain(dve.tensor_scalar(eps1[:, :], eps1[:, :], 1.0, None, ALU.add))
            over_blocks(dve, nodes0, 7)

            def shift_of(n, b):
                k = b * BATCH % HALF
                dve.wait_ge(pairs_ready, n + 1)
                dve.scalar_tensor_tensor(shift[:, :], twins[:, b % 2, :], 0.0,
                                         flag_chunk1[:, b * BATCH // HALF, SPARE, k:k + BATCH],
                                         ALU.is_gt, ALU.mult).then_inc(shift_made, 1)

            def target_of(n, b, first):
                k = b * BATCH % HALF
                dve.wait_ge(shift_made, n + 1)
                if not first:
                    dve.wait_ge(table_free, (n - 2) * BATCH)
                dve.tensor_tensor(target[:, b % SLOTS, :], shift[:, :],
                                  flag_chunk1[:, b * BATCH // HALF, TARGET, k:k + BATCH], ALU.add)\
                    .then_inc(target_ready, 1)

            def iteration1(i, first):
                for b in range(ITER_BATCHES):
                    r, h = b % SLOTS, b * BATCH // HALF
                    n = i * ITER_BATCHES + b
                    if b * BATCH % HALF == 0:
                        dve.wait_ge(flag_ready[1], 2 * i + h + 1)
                        dve.tensor_tensor(flag_chunk1[:, h, TARGET], flag_chunk1[:, h, SRC], table_row[:, :], ALU.add)
                    if not first or b >= 2:
                        dve.wait_ge(combined_ready, 2 * (n - 1))
                    dve.wait_ge(start_ready, n + 1)
                    dve.wait_ge(sources_copied, n + 1)
                    for s in range(BATCH):
                        k = (b * BATCH + s) % HALF
                        if not (first and b == 0 and s == 0):
                            dve.wait_ge(folded[1], n * BATCH + s)
                        dve.scalar_tensor_tensor(sring[:, r * BATCH + s, :],
                                                 sring[:, (r * BATCH + s - 1) % (SLOTS * BATCH), :],
                                                 flag_chunk1[:, h, KEEP, k:k + 1], started(b % 2, s),
                                                 ALU.mult, ALU.add).then_inc(folded[1], 1)
                        dve.tensor_scalar(pairs[:, b % 2, s, :], sources[:, b % 2, s], flag_chunk1[:, h, SRC, k:k + 1],
                                          flag_chunk1[:, h, WEIGHT, k:k + 1], ALU.is_equal, ALU.mult)
                        last = dve.scalar_tensor_tensor(pair_waste[:, b % 2, s], sources[:, b % 2, s],
                                                        flag_chunk1[:, h, SRC, k:k + 1],
                                                        before_me[:, :], ALU.is_equal, ALU.mult,
                                                        accum_out=twins[:, b % 2, s:s + 1])
                        if s == 0 and not (first and b == 0):
                            shift_of(n - 1, (b - 1) % ITER_BATCHES)
                        if s == 1 and not (first and b == 0):
                            target_of(n - 1, (b - 1) % ITER_BATCHES, first and b <= SLOTS)
                    last.then_inc(pairs_ready, 1)
                    if b == 4:
                        dve.tensor_tensor(blk(x_sb, i), blk(x_sb, i), off_rows[:, :], ALU.add).then_inc(side_done, 1)
            dve.wait_ge(start_gathered, 16)
            iteration1(0, True)
            with dve.Fori(1, ITERS) as i:
                iteration1(i, False)
            shift_of(CP // BATCH - 1, ITER_BATCHES - 1)
            target_of(CP // BATCH - 1, ITER_BATCHES - 1, False)
            dve.wait_ge(side_done, ITERS)

            def nodes1(t, b, g):
                if live(t, 3):
                    u, c = at(t, 3), (b - 3) % GROUP
                    dve.wait_ge(halved, u + 1)
                    if later(u, GROUP):
                        dve.wait_ge(n_turned[1], u - GROUP + 1)
                    dve.tensor_tensor(rows_u[:, c, :], block_sums[:, c, 0], block_sums[:, c, 1], ALU.add)\
                        .then_inc(n_comb[1], 1)
                if live(t, 6):
                    inverse_of(n_root[1], n_inverse[1], at(t, 6), (b - 6) % GROUP)
                if live(t, 7):
                    u, c = at(t, 7), (b - 7) % GROUP
                    dve.wait_ge(n_norm[1], u + 1)
                    if later(u, GROUP):
                        dve.wait_ge(rows_stored[c], 2 * STORED + 16 * uses(g, b, 7))
                    dve.tensor_tensor(rows_h[:, c, :], rows_n[:, c, :], scale_rows[:, :], ALU.mult).then_inc(n_scaled, 1)
                if live(t, 6):
                    shift_by_mean(n_inverse[1], n_ln[1], at(t, 6), (b - 6) % GROUP)
                if live(t, 5):
                    u, c = at(t, 5), (b - 5) % GROUP
                    dve.wait_ge(n_evac[1], u + 1)
                    sums_of(rows_n[:, c, :], n_stat[1], u, c)
                if live(t, 7):
                    u, c = at(t, 7), (b - 7) % GROUP
                    dve.wait_ge(n_scaled, u + 1)
                    dve.tensor_tensor(rows_h[:, c, :], rows_h[:, c, :], blk(x_sb, u), ALU.add).then_inc(n_out, 1)
                if live(t, 5):
                    moments(n_stat[1], at(t, 5), (b - 5) % GROUP)
            over_blocks(dve, nodes1, 7)


_INS = ['x', 'src', 'dst', 'edge_weight', 'L0_gnn_theta_w', 'L0_gnn_theta_b', 'L0_gnn_phi_w', 'L0_gnn_phi_b',
        'L1_gnn_W1', 'L1_gnn_b1', 'L1_gnn_W2', 'L1_gnn_b2', 'L1_gnn_eps', 'L1_gnn_offset', 'L1_gnn_scale']


def kernel(**inputs):
    import numpy as _np
    import concourse.bacc as _bacc
    from concourse import mybir as _mybir
    from concourse.bass_utils import run_bass_kernel_spmd as _run

    nc = _bacc.Bacc("TRN2", target_bir_lowering=False, num_devices=1)
    arrays, args = {}, []
    for name in _INS:
        a = _np.ascontiguousarray(inputs[name])
        arrays[f"in_{name}"] = a
        args.append(nc.dram_tensor(f"in_{name}", a.shape, _mybir.dt.from_np(a.dtype), kind="ExternalInput").ap())
    out = nc.dram_tensor("out_x", inputs['x'].shape, _mybir.dt.float32, kind="ExternalOutput").ap()
    two_gnn_layers(nc, *args, out)
    r = _run(nc, [arrays], core_ids=[0])
    return r.results[0]["out_x"]
```
